# Optimizing a Trainium2 kernel written in Bass

```python
import numpy as np
import jax
import jax.numpy as jnp

def _softmax(x, axis=-1):
    return jax.nn.softmax(x, axis=axis)

def _gelu(x):
    return jax.nn.gelu(x, approximate=True)

def _silu(x):
    return jax.nn.silu(x)

def _sigmoid(x):
    return jax.nn.sigmoid(x)

def _layernorm(x, axis=-1, eps=1e-05):
    m = jnp.mean(x, axis=axis, keepdims=True)
    v = jnp.var(x, axis=axis, keepdims=True)
    return (x - m) / jnp.sqrt(v + eps)

def _scatter_add(tgt, idx, src, axis=0):
    return tgt.at[idx].add(src)

def _segment_sum(src, seg, n):
    return jax.ops.segment_sum(src, seg, n)
kernel_name = 'mk_prb_d1_jaxref_r8_a1d580'

def setup_inputs(seed: int=0):
    np.random.seed(seed)
    _w = jnp.asarray

    def _L0_attn_setup():
        import jax, jax.numpy as jnp
        import numpy as np
        N_EMBED = 256
        N_HEAD = 16
        HEAD_DIM = N_EMBED // N_HEAD
        BATCH, SEQ = (2, 256)

        def _rotate_half(t):
            d = t.shape[-1] // 2
            x1, x2 = (t[..., :d], t[..., d:])
            return jnp.concatenate([-x2, x1], axis=-1)
        key = jax.random.key(seed)
        k1, k2, k3 = jax.random.split(key, 3)
        x = jax.random.normal(k1, (BATCH, SEQ, N_EMBED), dtype=jnp.float32)
        w_attn = jax.random.normal(k2, (N_EMBED, (N_HEAD + 2) * HEAD_DIM), dtype=jnp.float32) * N_EMBED ** (-0.5)
        w_out = jax.random.normal(k3, (N_EMBED, N_EMBED), dtype=jnp.float32) * N_EMBED ** (-0.5)
        return {'x': x, 'w_attn': w_attn, 'w_out': w_out}
    _L0_attn_in = _L0_attn_setup()

    def _L0_ffn_setup():
        import jax, jax.numpy as jnp
        import numpy as np
        TOP_K = 8
        NUM_EXPERTS = 32
        key = jax.random.key(seed)
        k1, k2, k3, k4, k5 = jax.random.split(key, 5)
        B, S, D, M, E = (4, 128, 256, 96, NUM_EXPERTS)
        return {'hidden_states': jax.random.normal(k1, (B, S, D), dtype=jnp.float32), 'gate_kernel': jax.random.normal(k2, (D, E), dtype=jnp.float32) * 0.02, 'gate_proj': jax.random.normal(k3, (E, D, M), dtype=jnp.float32) * 0.02, 'up_proj': jax.random.normal(k4, (E, D, M), dtype=jnp.float32) * 0.02, 'down_proj': jax.random.normal(k5, (E, M, D), dtype=jnp.float32) * 0.02}
    _L0_ffn_in = _L0_ffn_setup()
    _d = {'L0_attn_x': _L0_attn_in['x'], 'L0_attn_w_attn': _L0_attn_in['w_attn'], 'L0_attn_w_out': _L0_attn_in['w_out'], 'L0_ffn_gate_kernel': _L0_ffn_in['gate_kernel'], 'L0_ffn_gate_proj': _L0_ffn_in['gate_proj'], 'L0_ffn_up_proj': _L0_ffn_in['up_proj'], 'L0_ffn_down_proj': _L0_ffn_in['down_proj']}
    _x0 = _d['L0_attn_x']
    _d['L0_attn_x'] = jax.random.normal(jax.random.fold_in(jax.random.key(seed), 1), (4, 512, 256), dtype=_x0.dtype)
    del _x0
    return _d

def reference(L0_attn_x, L0_attn_w_attn, L0_attn_w_out, L0_ffn_gate_kernel, L0_ffn_gate_proj, L0_ffn_up_proj, L0_ffn_down_proj):

    def _L0_attn_ref(x, w_attn, w_out):
        import jax, jax.numpy as jnp
        import numpy as np
        N_EMBED = 256
        N_HEAD = 16
        HEAD_DIM = N_EMBED // N_HEAD
        BATCH, SEQ = (2, 256)

        def _rotate_half(t):
            d = t.shape[-1] // 2
            x1, x2 = (t[..., :d], t[..., d:])
            return jnp.concatenate([-x2, x1], axis=-1)
        B, T, E = x.shape
        H, hd = (N_HEAD, HEAD_DIM)
        qkv = x @ w_attn
        q = qkv[..., :H * hd].reshape(B, T, H, hd).transpose(0, 2, 1, 3)
        k = qkv[..., H * hd:(H + 1) * hd].reshape(B, T, 1, hd).transpose(0, 2, 1, 3)
        v = qkv[..., (H + 1) * hd:].reshape(B, T, 1, hd).transpose(0, 2, 1, 3)
        pos = 10000.0 ** ((-2.0 * jnp.arange(0, hd, 2, dtype=jnp.float32) - 1.0) / hd)
        angles = jnp.arange(T, dtype=jnp.float32)[:, None] * pos[None, :]
        rot = jnp.concatenate([angles, angles], axis=-1)
        cos, sin = (jnp.cos(rot), jnp.sin(rot))
        q = q * cos + _rotate_half(q) * sin
        k = k * cos + _rotate_half(k) * sin
        scores = jnp.matmul(q, jnp.swapaxes(k, -1, -2)) * hd ** (-0.5)
        attn = jax.nn.softmax(scores, axis=-1)
        out = jnp.matmul(attn, v)
        out = out.transpose(0, 2, 1, 3).reshape(B, T, E)
        return out @ w_out

    def _L0_ffn_ref(hidden_states, gate_kernel, gate_proj, up_proj, down_proj):
        import jax, jax.numpy as jnp
        import numpy as np
        TOP_K = 8
        NUM_EXPERTS = 32
        B, S, D = hidden_states.shape
        T = B * S
        x2d = hidden_states.reshape(T, D)
        router_logits = x2d @ gate_kernel
        routing_weights = jax.nn.softmax(router_logits, axis=-1)
        routing_weights, selected_experts = jax.lax.top_k(routing_weights, TOP_K)
        routing_weights = routing_weights / jnp.sum(routing_weights, axis=-1, keepdims=True)
        flat_experts = selected_experts.reshape(-1)
        sort_idx = jnp.argsort(flat_experts)
        token_rows = sort_idx // TOP_K
        sorted_inputs = jnp.take(x2d, token_rows, axis=0)
        group_sizes = jnp.bincount(flat_experts, length=NUM_EXPERTS).astype(jnp.int32)
        w0 = jax.lax.ragged_dot(sorted_inputs, gate_proj, group_sizes, preferred_element_type=jnp.float32)
        w1 = jax.lax.ragged_dot(sorted_inputs, up_proj, group_sizes, preferred_element_type=jnp.float32)
        inter = jax.nn.silu(w0) * w1
        expert_out = jax.lax.ragged_dot(inter, down_proj, group_sizes, preferred_element_type=jnp.float32)
        unsorted = jnp.take(expert_out, jnp.argsort(sort_idx), axis=0)
        per_token = unsorted.reshape(T, TOP_K, D)
        output = jnp.einsum('BKE,BK->BE', per_token.astype(jnp.float32), routing_weights.astype(jnp.float32))
        return output.reshape(B, S, D)
    x = L0_attn_x
    xn = _layernorm(x, axis=-1)
    x = x + _L0_attn_ref(xn, L0_attn_w_attn, L0_attn_w_out) + _L0_ffn_ref(xn, L0_ffn_gate_kernel, L0_ffn_gate_proj, L0_ffn_up_proj, L0_ffn_down_proj)
    return x

_drawn_inputs = setup_inputs


def setup_inputs(seed=0):
    import zlib

    import numpy as np

    out = dict(_drawn_inputs(seed))
    spreads = {}
    factors = {'L0_ffn_gate_kernel': 8.0,
     'L0_ffn_gate_proj': 8.0,
     'L0_ffn_up_proj': 8.0,
     'L0_ffn_down_proj': 8.0,
     'L0_attn_w_out': 2.686}
    for name, (base, spread) in spreads.items():
        noise = np.random.default_rng([zlib.crc32(name.encode()), seed]).standard_normal(out[name].shape)
        drawn = base * np.exp(spread * noise) if base else spread * noise
        out[name] = jnp.asarray(drawn.astype(out[name].dtype))
    for name, factor in factors.items():
        out[name] = (out[name] * factor).astype(out[name].dtype)
    return out
```

```python
from contextlib import ExitStack

import numpy as np

import concourse.bass as bass
from concourse import mybir

F32 = mybir.dt.float32
F32R = mybir.dt.float32r
BF16 = mybir.dt.bfloat16
FP16 = mybir.dt.float16
ALU = mybir.AluOpType
ACT = mybir.ActivationFunctionType
AX = mybir.AxisListType

P = 128
NB, T, D = 4, 512, 256
BLK = T // P
DC = D // P
H, HD = 16, 16
HALF = HD // 2
NQK = (H + 1) * HD
NQKV = (H + 2) * HD
E, M, TOPK = 32, 96, 8
NPROJ = NQKV + E
HID = E * M
NCH = HID // P
GE = 4
GH = GE * M
GC = GH // P
NG = E // GE
HS = 64
KS = 3 * HD
KM = KS + 2
PAIRS = H // 2
VW = 32
SCALE = HD ** -0.5
EPS = 1e-5

STEPS = ["norm", "xT0", "xT1", "proj0", "proj1", "proj2", "proj3", "rope", "route", "kT", "wT", "qT0", "qT1"]
for _p in range(PAIRS):
    for _s in range(2 * BLK):
        STEPS.append(f"S{_p}.{_s}")
        if _s == 3 and _p:
            STEPS.append(f"qmT{_p - 1}")
        if _s == 5 and 1 <= _p < PAIRS - 1:
            STEPS.append(f"qT{_p + 1}")
STEPS.append(f"qmT{PAIRS - 1}")
RING = {name: n for n, name in enumerate(s for s in STEPS if s not in ("norm", "rope", "route"))}
assert len(RING) % 2 == 0
RING_PER = len(RING) // 2
MISC_PER = H + 2 * DC

POINTS = ["sT01", "pv0a", "pv0b", "sT23", "pv1a", "pv1b", "turn"]
FIRST = {"norm": 0, "xT0": 4, "xT1": 4, "proj0": 6, "proj1": 6, "proj2": 7, "proj3": 7, "rope": 8,
         "route": 10, "kT": 13, "wT": 13, "qT0": 14, "qT1": 14}


def front_plan():
    plan = {n: [] for n in range(len(POINTS) * (PAIRS + 1))}
    for name in STEPS[:len(FIRST)]:
        plan[FIRST[name]].append(name)
    for n, name in enumerate(STEPS[len(FIRST):-1]):
        plan[15 + n // 2].append(name)
    plan[len(plan) - 2].append(STEPS[-1])
    return plan


PLAN = front_plan()


def program(nc, x, w_attn, w_out, gate_kernel, gate_proj, up_proj, down_proj, cos, sin, ident, sel, out):
    down_rows = down_proj.rearrange("e m d -> (e m) d")
    xT_dram = nc.dram_tensor("xT_spill", (NB, P, 2 * DC * T), F32, kind="Internal").ap()
    acc_dram = nc.dram_tensor("acc_spill", (NB, P, BLK * D), F32, kind="Internal").ap()

    with ExitStack() as ctx:
        def sb(name, shape, dt=F32, where=ctx):
            return where.enter_context(nc.sbuf_tensor(name, shape, dt))

        def psum(name, shape):
            return ctx.enter_context(nc.psum_tensor(name, shape, F32))

        def sems(names):
            return [ctx.enter_context(nc.semaphore(name)) for name in names.split()]

        identf = sb("identf", [P, P])
        identb = sb("identb", [P, P], BF16)
        sel_sb = sb("sel_sb", [3 * E, HID], FP16)
        wT3 = sb("wT3", [3 * E, NB * T], BF16)
        stage = sb("stage", [P, 3, DC * GH])
        w_raw = stage[:].rearrange("p s n -> p (s n)")[:, 0:DC * (NPROJ + D)].rearrange("p (c n) -> p c n", c=DC)
        g_hi, g_lo = sb("g_hi", [P, DC, HID], F32R), sb("g_lo", [P, DC, HID], F32R)

        ph1 = ExitStack()
        cs = sb("cs", [P, 2, BLK, HD], where=ph1)
        wa_hi, wa_lo = (sb(n, [P, DC, NPROJ], F32R, ph1) for n in ("wa_hi", "wa_lo"))
        wo_hi, wo_lo = (sb(n, [P, DC, D], F32R, ph1) for n in ("wo_hi", "wo_lo"))
        xs = sb("xs", [P, BLK, D], where=ph1)
        xn = sb("xn", [P, BLK, D], where=ph1)
        bn = sb("bn", [P, BLK, 6], where=ph1)
        mv = sb("mv", [P, BLK, 2], where=ph1)
        veps = sb("veps", [P, BLK], where=ph1)
        rstd = sb("rstd", [P, BLK], where=ph1)
        mhalf = sb("mhalf", [P, BLK], where=ph1)
        xT = sb("xT", [P, 2, DC, T], F32R, ph1)
        qkv = sb("qkv", [P, BLK, NPROJ], where=ph1)
        rot_c = sb("rot_c", [P, BLK, NQK], where=ph1)
        rot_s = sb("rot_s", [P, BLK, NQK], where=ph1)
        qa = sb("qa", [P, BLK, H, HS], where=ph1)
        ka = sb("ka", [P, BLK, 2, HS], where=ph1)
        kT_new = sb("kT_new", [P, T], F32R, ph1)
        kT_cur = sb("kT_cur", [P, T], F32R, ph1)
        v_new = sb("v_new", [P, BLK, VW], where=ph1)
        v_cur = sb("v_cur", [P, BLK, VW], where=ph1)
        qT = sb("qT", [P, 2, T], F32R, ph1)
        qmT = sb("qmT", [P, PAIRS, T], F32R, ph1)
        nmax = sb("nmax", [P, 2, BLK, 2], where=ph1)
        lmax = sb("lmax", [P, BLK], where=ph1)
        ex = sb("ex", [P, BLK, E], where=ph1)
        top8 = sb("top8", [P, BLK, TOPK], where=ph1)
        rest = sb("rest", [P, BLK, E], where=ph1)
        nsum = sb("nsum", [P, BLK], where=ph1)
        nrec = sb("nrec", [P, BLK], where=ph1)
        wgt = sb("wgt", [P, BLK, E], where=ph1)
        w3 = sb("w3", [P, BLK, 3 * E], BF16, ph1)
        probs = sb("probs", [P, 2, BLK, 2, T], where=ph1)
        pvs = sb("pvs", [P, 2, T], where=ph1)
        ov = sb("ov", [P, 2, BLK, HD + 1], where=ph1)
        orec = sb("orec", [P, 2, BLK], where=ph1)
        o_tok = sb("o_tok", [P, BLK, D], where=ph1)
        oT = sb("oT", [P, 2, DC, T], F32R, ph1)
        acc = sb("acc", [P, BLK, D], where=ph1)
        ph1.close()

        u_hi, u_lo = sb("u_hi", [P, DC, HID], F32R), sb("u_lo", [P, DC, HID], F32R)
        d_hi, d_lo = sb("d_hi", [P, NCH, D], F32R), sb("d_lo", [P, NCH, D], F32R)
        xT2 = sb("xT2", [P, 2, DC, T], F32R)
        act_g = sb("act_g", [P, 2, T])
        hid = sb("hid", [P, 2, T])
        h_hi, h_lo = sb("h_hi", [P, 2, T], F32R), sb("h_lo", [P, 2, T], F32R)
        dT = sb("dT", [P, DC, T])
        acc2 = sb("acc2", [P, BLK, D])

        ring = [psum(f"ring{i}", [P, T]) for i in range(2)]
        sT = [psum(f"sT{i}", [P, 2, T]) for i in range(2)]
        pv, misc = psum("pv", [P, T]), psum("misc", [P, T])
        gate_ps, up_ps, down_ps, wgt_ps, turn_ps = ring, (sT[0][:, 0, :], sT[0][:, 1, :]), sT[1], pv, misc

        consts_in, w_in, wa_hi_done, wo_hi_done, wa_split, wo_split, fixed, identb_done = sems(
            "consts_in w_in wa_hi_done wo_hi_done wa_split wo_split fixed identb_done")
        (waited_apart,) = sems("waited_apart")
        x_in, bn_done, mv_done, veps_done, rstd_done, xn_done, xThi_done, xT_out = sems(
            "x_in bn_done mv_done veps_done rstd_done xn_done xThi_done xT_out")
        ring_full, ring_taken = sems("ring_full0 ring_full1"), sems("ring_taken0 ring_taken1")
        rotc_done, rots_done, rot_done, qhi_done, qa_done, khi_done, ka_done, v_done, kv_cur = sems(
            "rotc_done rots_done rot_done qhi_done qa_done khi_done ka_done v_done kv_cur")
        lmax_done, lsub_done, ex_done, top8_done, rest_done, nsum_done, nrec_done, selneg_done, wgt_done = sems(
            "lmax_done lsub_done ex_done top8_done rest_done nsum_done nrec_done selneg_done wgt_done")
        w3a_done, w3r_done, w3b_done, w3_done, mhi_done, m_done = sems(
            "w3a_done w3r_done w3b_done w3_done mhi_done m_done")
        sT_full, exp_done, pv_full, pvs_done, misc_full, misc_taken, orec_done, norm_done, oThi_done = sems(
            "sT_full exp_done pv_full pvs_done misc_full misc_taken orec_done norm_done oThi_done")
        acc_in, acc_out = sems("acc_in acc_out")
        stage_in = sems("stage_in0 stage_in1 stage_in2")
        hi_done, lo_done = sems("hi_done lo_done")
        xT2_in, acc2_in, gate_full, up_full, wps_full, silu_done, gu_done, hid_done, hhi_done, hlo_done = sems(
            "xT2_in acc2_in gate_full up_full wps_full silu_done gu_done hid_done hhi_done hlo_done")
        down_used, dT_done, turn_full, turn_taken, out_done = sems(
            "down_used dT_done turn_full turn_taken out_done")

        def ring_at(name):
            n = RING[name]
            return ring[n % 2], ring_full[n % 2], ring_taken[n % 2], n // 2

        def ring_wait(eng, which, j, name, done=1):
            n = RING[name]
            eng.wait_ge(which[n % 2], RING_PER * j + n // 2 + done)

        def both_phases(eng, back, front, tail):
            def step(i, j):
                for n in range(len(POINTS) * (PAIRS + 1)):
                    if i is not None:
                        back(i, n // len(POINTS), POINTS[n % len(POINTS)])
                    if j is not None:
                        for name in PLAN[n]:
                            front(i, j, name)
                if i is not None:
                    tail(i)

            step(None, 0)
            step(0, 1)
            with eng.Fori(1, NB - 1) as i:
                step(i, i + 1)
            step(NB - 1, None)

        groups = [("g", g) for g in range(NG)]
        for g in range(NG):
            groups += [("u", g), ("d", g)]
        order = {key: n for n, key in enumerate(groups)}

        def wait_apart(eng, semaphore, value):
            eng.wait_ge(semaphore, value)
            eng.sem_inc(waited_apart, 1)

        block = ctx.enter_context(nc.Block())

        @block.sync
        def _(sp):
            def tok(a, b):
                return a[bass.ds(b, 1), :, :].rearrange("o (b p) d -> p (o b) d", p=P)

            def row(a, b):
                return a[bass.ds(b, 1), :, :].rearrange("o p n -> p (o n)")

            def load_x(j):
                sp.wait_ge(xn_done, BLK * j)
                sp.dma_start(xs[:], tok(x, j)).then_inc(x_in, 16)

            def load_group(n):
                kind, g = groups[n]
                if n >= 3:
                    sp.wait_ge(lo_done, n - 2)
                slot = stage[:, n % 3, :]
                if kind == "d":
                    to = slot.rearrange("p (r d) -> p r d", r=GC)
                    rows = down_rows[g * GH:(g + 1) * GH, :].rearrange("(r p) d -> p r d", p=P)
                    sp.dma_start(to[:, 0:2, :], rows[:, 0:2, :]).then_inc(stage_in[n % 3], 16)
                    sp.dma_start(to[:, 2:GC, :], rows[:, 2:GC, :]).then_inc(stage_in[n % 3], 16)
                else:
                    w = gate_proj if kind == "g" else up_proj
                    for c in range(DC):
                        sp.dma_start(slot[:, c * GH:(c + 1) * GH].rearrange("p (e m) -> p e m", e=GE),
                                     w[g * GE:(g + 1) * GE, c * P:(c + 1) * P, :].rearrange("e p m -> p e m")
                                     ).then_inc(stage_in[n % 3], 16)

            def load_residual(i):
                sp.wait_ge(acc_out, 16 * i)
                sp.dma_start(acc[:], tok(x, i)).then_inc(acc_in, 16)

            def spill_xT(j):
                ring_wait(sp, ring_taken, j, "xT0")
                ring_wait(sp, ring_taken, j, "xT1")
                sp.dma_start(row(xT_dram, j), xT[:].rearrange("p a c t -> p (a c t)").bitcast(F32)).then_inc(xT_out, 16)

            def spill_acc(i):
                sp.wait_ge(misc_taken, MISC_PER * i + MISC_PER)
                sp.dma_start(row(acc_dram, i), acc[:].rearrange("p b d -> p (b d)")).then_inc(acc_out, 16)

            sp.dma_start(xs[:], tok(x, 0)).then_inc(x_in, 16)
            sp.dma_start(w_raw[:, :, 0:NQKV], w_attn.rearrange("(c p) n -> p c n", p=P)).then_inc(w_in, 16)
            sp.dma_start(w_raw[:, :, NQKV:NPROJ], gate_kernel.rearrange("(c p) n -> p c n", p=P)).then_inc(w_in, 16)
            sp.dma_start(identf[:], ident).then_inc(consts_in, 16)
            sp.dma_start(cs[:, 0, :, :], cos).then_inc(consts_in, 16)
            sp.dma_start(cs[:, 1, :, :], sin).then_inc(consts_in, 16)
            sp.dma_start(w_raw[:, :, NPROJ:NPROJ + D], w_out.rearrange("(c p) n -> p c n", p=P)).then_inc(w_in, 16)
            sp.dma_start(sel_sb[:], sel).then_inc(consts_in, 16)
            sp.dma_start(acc[:], tok(x, 0)).then_inc(acc_in, 16)
            load_x(1)
            spill_xT(0)
            sp.wait_ge(wo_split, 1)
            for n in range(NG):
                load_group(n)
            with sp.Fori(0, NB - 2) as i:
                load_x(i + 2)
                spill_xT(i + 1)
                spill_acc(i)
                load_residual(i + 1)
            spill_xT(NB - 1)
            spill_acc(NB - 2)
            load_residual(NB - 1)
            for n in range(NG, NG + 3):
                load_group(n)
            spill_acc(NB - 1)

            def load_batch(b):
                sp.wait_ge(up_full, NCH * b)
                sp.dma_start(xT2[:].rearrange("p a c t -> p (a c t)").bitcast(F32), row(xT_dram, b)).then_inc(xT2_in, 16)

            def load_acc(b):
                sp.wait_ge(out_done, 32 * b)
                sp.dma_start(acc2[:].rearrange("p b d -> p (b d)"), row(acc_dram, b)).then_inc(acc2_in, 16)

            def store(b):
                for half in range(2):
                    sp.wait_ge(turn_taken, 2 * b + half + 1)
                    sp.dma_start(tok(out, b)[:, 2 * half:2 * half + 2, :],
                                 acc2[:, 2 * half:2 * half + 2, :]).then_inc(out_done, 16)

            sp.wait_ge(xT_out, 16 * NB)
            sp.wait_ge(acc_out, 16 * NB)
            load_batch(0)
            for n in range(NG + 3, len(groups)):
                load_group(n)
                if n == NG + 5:
                    sp.dma_start(acc2[:].rearrange("p b d -> p (b d)"), row(acc_dram, 0)).then_inc(acc2_in, 16)
            with sp.Fori(0, NB - 1) as b:
                load_batch(b + 1)
                store(b)
                load_acc(b + 1)
            store(NB - 1)
            sp.wait_ge(out_done, 32 * NB)

        @block.gpsimd
        def _(pool):
            nc.gpsimd.memset(mhalf[:], -0.5).then_inc(fixed, 1)
            nc.gpsimd.memset(qa[:].rearrange("p b h s -> p (b h) s")[:, :, KS:HS], 0.0).then_inc(fixed, 1)
            kav = ka[:].rearrange("p b t s -> p (b t) s")
            nc.gpsimd.memset(kav[:, :, KS:KM], 1.0).then_inc(fixed, 1)
            nc.gpsimd.memset(kav[:, :, KM:HS], 0.0).then_inc(fixed, 1)
            nc.gpsimd.memset(v_new[:, :, HD:HD + 1], 1.0).then_inc(fixed, 1)
            nc.gpsimd.memset(v_new[:, :, HD + 1:VW], 0.0).then_inc(fixed, 1)

            def norm(j):
                wait_apart(pool, mv_done, BLK * j + BLK)
                nc.gpsimd.tensor_scalar(veps[:], mv[:, :, 1], EPS, None, ALU.add).then_inc(veps_done, 1)
                pool.wait_ge(veps_done, j + 1)
                pool.wait_ge(xn_done, BLK * j)
                nc.gpsimd.tensor_tensor(rstd[:], veps[:], mhalf[:], ALU.pow).then_inc(rstd_done, 1)

            def rope(j):
                rot = rot_c[:].rearrange("p b (h d) -> p b h d", d=HD)
                q, k = rot[:, :, 0:H, :], rot[:, :, H, :].unsqueeze(2).to_broadcast([P, BLK, 2, HD])
                pool.wait_ge(ring_full[0], RING_PER * j)
                pool.wait_ge(ring_full[1], RING_PER * j)
                wait_apart(pool, rot_done, j + 1)
                nc.gpsimd.tensor_copy(ka[:, :, :, 0:HD].bitcast(F32R), k).then_inc(khi_done, 1)
                nc.gpsimd.tensor_copy(ka[:, :, :, 2 * HD:3 * HD].bitcast(F32R), k).then_inc(khi_done, 1)
                nc.gpsimd.tensor_copy(qa[:, :, :, 0:HD].bitcast(F32R), q).then_inc(qhi_done, 1)
                pool.wait_ge(khi_done, 2 * j + 2)
                nc.gpsimd.tensor_tensor(ka[:, :, :, HD:2 * HD].bitcast(F32R), k, ka[:, :, :, 0:HD],
                                        ALU.subtract).then_inc(ka_done, 1)
                nc.gpsimd.tensor_copy(qa[:, :, :, HD:2 * HD].bitcast(F32R), q).then_inc(qhi_done, 1)
                pool.wait_ge(qhi_done, 2 * j + 1)
                nc.gpsimd.tensor_tensor(qa[:, :, :, 2 * HD:3 * HD].bitcast(F32R), q, qa[:, :, :, 0:HD],
                                        ALU.subtract).then_inc(qa_done, 1)

            def route(j):
                ring_wait(pool, ring_full, j, "wT", 0)
                wait_apart(pool, wgt_done, j + 1)
                nc.gpsimd.tensor_copy(w3[:, :, 0:E], wgt[:]).then_inc(w3a_done, 1)
                pool.wait_ge(w3a_done, j + 1)
                nc.gpsimd.tensor_tensor(ex[:], wgt[:], w3[:, :, 0:E], ALU.subtract).then_inc(w3r_done, 1)
                wait_apart(pool, w3r_done, j + 1)
                nc.gpsimd.tensor_copy(w3[:, :, E:2 * E], ex[:]).then_inc(w3b_done, 1)
                pool.wait_ge(w3b_done, j + 1)
                nc.gpsimd.tensor_tensor(w3[:, :, 2 * E:3 * E], ex[:], w3[:, :, E:2 * E], ALU.subtract).then_inc(w3_done, 1)

            def take_kv(i):
                ring_wait(pool, ring_taken, i, "kT")
                pool.wait_ge(v_done, i + 1)
                wait_apart(pool, pv_full, H * i)
                nc.gpsimd.tensor_copy(kT_cur[:], kT_new[:].bitcast(F32)).then_inc(kv_cur, 1)
                nc.gpsimd.tensor_copy(v_cur[:], v_new[:]).then_inc(kv_cur, 1)

            def split_group(n):
                kind, g = groups[n]
                w_hi, w_lo = {"g": (g_hi, g_lo), "u": (u_hi, u_lo), "d": (d_hi, d_lo)}[kind]

                def at(w):
                    return w[:, g * GC:(g + 1) * GC, :] if kind == "d" else w[:, :, g * GH:(g + 1) * GH]

                src = stage[:, n % 3, :].rearrange("p (r d) -> p r d", r=GC if kind == "d" else DC)
                pool.wait_ge(stage_in[n % 3], 32 * (n // 3 + 1))
                nc.gpsimd.tensor_copy(at(w_hi), src).then_inc(hi_done, 1)
                pool.wait_ge(hi_done, n + 1)
                nc.gpsimd.tensor_tensor(at(w_lo), src, at(w_hi).bitcast(F32), ALU.subtract).then_inc(lo_done, 1)

            pool.wait_ge(w_in, 48)
            nc.gpsimd.tensor_copy(wa_hi[:], w_raw[:, :, 0:NPROJ]).then_inc(wa_hi_done, 1)
            pool.wait_ge(wa_hi_done, 1)
            nc.gpsimd.tensor_tensor(wa_lo[:], w_raw[:, :, 0:NPROJ], wa_hi[:].bitcast(F32), ALU.subtract).then_inc(wa_split, 1)
            norm(0)
            nc.gpsimd.tensor_copy(wo_hi[:], w_raw[:, :, NPROJ:NPROJ + D]).then_inc(wo_hi_done, 1)
            pool.wait_ge(wo_hi_done, 1)
            nc.gpsimd.tensor_tensor(wo_lo[:], w_raw[:, :, NPROJ:NPROJ + D], wo_hi[:].bitcast(F32), ALU.subtract).then_inc(wo_split, 1)
            rope(0)
            route(0)
            for n in range(NG):
                split_group(n)

            def next_batch(i):
                take_kv(i)
                norm(i + 1)
                rope(i + 1)
                route(i + 1)

            next_batch(0)
            with pool.Fori(1, NB - 1) as i:
                next_batch(i)
            take_kv(NB - 1)

            def hidden_lo(b, c):
                pool.wait_ge(hhi_done, NCH * b + c + 1)
                pool.wait_ge(down_used, NCH * b + max(c - 1, 0))
                nc.gpsimd.tensor_tensor(h_lo[:, c % 2, :], hid[:, c % 2, :], h_hi[:, c % 2, :].bitcast(F32),
                                        ALU.subtract).then_inc(hlo_done, 1)

            pool.wait_ge(acc_out, 16 * NB)
            pool.wait_ge(xT_out, 16 * NB)
            for g in range(NG):
                split_group(order["u", g])
                split_group(order["d", g])
                for c in range(max(GC * (g - 1), 0), GC * g):
                    hidden_lo(0, c)
            for c in range(NCH - GC, NCH):
                hidden_lo(0, c)
            with pool.Fori(1, NB) as b:
                for c in range(NCH):
                    hidden_lo(b, c)

        @block.scalar
        def _(act):
            def take(j, name, dst, src=None):
                bank, full, taken, k = ring_at(name)
                act.wait_ge(full, RING_PER * j + k + 1)
                nc.scalar.activation(dst, bank[:] if src is None else src(bank), ACT.Copy).then_inc(taken, 1)

            def front(i, j, name):
                if name.startswith("xT"):
                    c = int(name[2:])
                    bank, full, taken, k = ring_at(name)
                    act.wait_ge(full, RING_PER * j + k + 1)
                    act.wait_ge(xT_out, 16 * j)
                    nc.scalar.activation(xT[:, 0, c, :], bank[:], ACT.Copy).then_inc(xThi_done, 1)
                elif name.startswith("proj"):
                    b = int(name[4:])
                    if b == 0:
                        act.wait_ge(w3_done, j)
                        act.wait_ge(v_done, j)
                    take(j, name, qkv[:, b, :], lambda bank: bank[:, 0:NPROJ])
                elif name == "rope":
                    ring_wait(act, ring_taken, j, "proj2")
                    ring_wait(act, ring_taken, j, "proj3")
                    act.wait_ge(kv_cur, 2 * j)
                    act.wait_ge(fixed, 6)
                    nc.scalar.activation(v_new[:, :, 0:HD], qkv[:, :, NQK:NQKV], ACT.Copy).then_inc(v_done, 1)
                elif name == "route":
                    act.wait_ge(lsub_done, j + 1)
                    nc.scalar.activation(ex[:], ex[:], ACT.Exp).then_inc(ex_done, 1)
                elif name == "kT":
                    act.wait_ge(kv_cur, 2 * j)
                    take(j, name, kT_new[:])
                elif name == "wT":
                    take(j, name, wT3[:, bass.ds(j * T, T)], lambda bank: bank[0:3 * E, 0:T // 2].bitcast(BF16))
                elif name.startswith("qT"):
                    take(j, name, qT[:, int(name[2:]) % 2, :])
                elif name.startswith("qmT"):
                    p = int(name[3:])
                    if i is not None:
                        act.wait_ge(sT_full, 4 * PAIRS * i + 4 * (p + 1))
                    take(j, name, qmT[:, p, :])

            def exp(i, p, kb):
                n = BLK * p + kb
                act.wait_ge(sT_full, 4 * PAIRS * i + n + 1)
                act.wait_ge(pv_full, H * i + 2 * max(p - 1, 0))
                nc.scalar.activation(probs[:, p % 2, kb, :, :], sT[n % 2][:], ACT.Exp, scale=SCALE).then_inc(exp_done, 1)

            def take_pv(i, n):
                act.wait_ge(pv_full, H * i + n + 1)
                act.wait_ge(misc_full, MISC_PER * i + max(n - 1, 0))
                nc.scalar.activation(pvs[:, n % 2, :], pv[:], ACT.Copy).then_inc(pvs_done, 1)

            def back(i, u, point):
                if u < PAIRS and point == "sT01":
                    exp(i, u, 0)
                    exp(i, u, 1)
                if u < PAIRS and point == "sT23":
                    exp(i, u, 2)
                    exp(i, u, 3)
                if u and point == "pv0b":
                    take_pv(i, 2 * (u - 1))
                if u and point == "pv1b":
                    take_pv(i, 2 * (u - 1) + 1)

            def tail(i):
                for c in range(DC):
                    act.wait_ge(misc_full, MISC_PER * i + H + c + 1)
                    nc.scalar.activation(oT[:, 0, c, :], misc[:], ACT.Copy).then_inc(oThi_done, 1)

            act.wait_ge(consts_in, 64)
            nc.scalar.activation(identb[:], identf[:], ACT.Copy).then_inc(identb_done, 1)
            both_phases(act, back, front, tail)

            def silu(b, c):
                act.wait_ge(gate_full, NCH * b + c + 1)
                act.wait_ge(gu_done, NCH * b + max(c - 1, 0))
                nc.scalar.activation(act_g[:, c % 2, :], gate_ps[c % 2][:], ACT.Silu).then_inc(silu_done, 1)

            def hidden_hi(b, c):
                act.wait_ge(hid_done, NCH * b + c + 1)
                act.wait_ge(down_used, NCH * b + max(c - 1, 0))
                nc.scalar.activation(h_hi[:, c % 2, :], hid[:, c % 2, :], ACT.Copy).then_inc(hhi_done, 1)

            def experts(b):
                for c in range(NCH + 1):
                    if c < NCH:
                        silu(b, c)
                    if c:
                        hidden_hi(b, c - 1)
                act.wait_ge(down_used, NCH * b + NCH)
                act.wait_ge(turn_full, 2 * b)
                nc.scalar.activation(dT[:, 0, :], down_ps[:, 0, :], ACT.Copy).then_inc(dT_done, 1)

            experts(0)
            with act.Fori(1, NB) as b:
                experts(b)

        @block.vector
        def _(dve):
            def front(i, j, name):
                if name == "norm":
                    dve.wait_ge(x_in, 16 * j + 16)
                    for b in range(BLK):
                        nc.vector.bn_stats(bn[:, b, :], xs[:, b, :]).then_inc(bn_done, 1)
                    dve.wait_ge(xn_done, BLK * j)
                    wait_apart(dve, bn_done, BLK * j + BLK)
                    for b in range(BLK):
                        nc.vector.bn_aggr(mv[:, b, :], bn[:, b, :]).then_inc(mv_done, 1)
                    dve.wait_ge(rstd_done, j + 1)
                    ring_wait(dve, ring_full, j, "xT0", 0)
                    ring_wait(dve, ring_full, j, "xT1", 0)
                    for b in range(BLK):
                        nc.vector.tensor_scalar(xn[:, b, :], xs[:, b, :], mv[:, b, 0:1], rstd[:, b:b + 1],
                                                ALU.subtract, ALU.mult).then_inc(xn_done, 1)
                elif name.startswith("xT"):
                    c = int(name[2:])
                    bank, full, taken, k = ring_at(name)
                    dve.wait_ge(xThi_done, DC * j + c + 1)
                    nc.vector.tensor_tensor(xT[:, 1, c, :], bank[:], xT[:, 0, c, :].bitcast(F32),
                                            ALU.subtract).then_inc(taken, 1)
                elif name == "rope":
                    ring_wait(dve, ring_taken, j, "proj2")
                    ring_wait(dve, ring_taken, j, "proj3")
                    dve.wait_ge(consts_in, 64)
                    dve.wait_ge(qa_done, j)
                    xv = qkv[:, :, 0:NQK].rearrange("p b (h d) -> p b h d", d=HD)
                    rc = rot_c[:].rearrange("p b (h d) -> p b h d", d=HD)
                    rs = rot_s[:].rearrange("p b (h d) -> p b h d", d=HD)

                    def table(which, lo, hi):
                        return cs[:, which, :, lo:hi].unsqueeze(2).to_broadcast([P, BLK, H + 1, hi - lo])

                    nc.vector.tensor_tensor(rc, xv, table(0, 0, HD), ALU.mult).then_inc(rotc_done, 1)
                    nc.vector.tensor_tensor(rs[:, :, :, 0:HALF], xv[:, :, :, HALF:HD], table(1, 0, HALF),
                                            ALU.mult).then_inc(rots_done, 1)
                    nc.vector.tensor_tensor(rs[:, :, :, HALF:HD], xv[:, :, :, 0:HALF], table(1, HALF, HD),
                                            ALU.mult).then_inc(rots_done, 1)
                    dve.wait_ge(rotc_done, j + 1)
                    dve.wait_ge(rots_done, 2 * j + 2)
                    nc.vector.tensor_tensor(rot_c[:], rot_c[:], rot_s[:], ALU.add).then_inc(rot_done, 1)
                elif name == "route":
                    logits = qkv[:, :, NQKV:NPROJ]
                    dve.wait_ge(w3_done, j)
                    nc.vector.tensor_reduce(lmax[:], logits, AX.X, ALU.max).then_inc(lmax_done, 1)
                    dve.wait_ge(lmax_done, j + 1)
                    nc.vector.tensor_tensor(ex[:], logits, lmax[:].unsqueeze(2).to_broadcast([P, BLK, E]),
                                            ALU.subtract).then_inc(lsub_done, 1)
                    wait_apart(dve, ex_done, j + 1)
                    for b in range(BLK):
                        nc.vector.max(top8[:, b, :], ex[:, b, :]).then_inc(top8_done, 1)
                    wait_apart(dve, top8_done, BLK * j + BLK)
                    for b in range(BLK):
                        nc.vector.match_replace(out=rest[:, b, :], in_to_replace=top8[:, b, :], in_values=ex[:, b, :],
                                                imm_value=-1.0).then_inc(rest_done, 1)
                    nc.vector.tensor_reduce(nsum[:], top8[:], AX.X, ALU.add, negate=True).then_inc(nsum_done, 1)
                    dve.wait_ge(nsum_done, j + 1)
                    nc.vector.reciprocal(nrec[:], nsum[:]).then_inc(nrec_done, 1)
                    dve.wait_ge(rest_done, BLK * j + BLK)
                    nc.vector.scalar_tensor_tensor(out=wgt[:], in0=rest[:], scalar=0.0, in1=ex[:], op0=ALU.max,
                                                   op1=ALU.subtract).then_inc(selneg_done, 1)
                    dve.wait_ge(nrec_done, j + 1)
                    dve.wait_ge(selneg_done, j + 1)
                    nc.vector.tensor_tensor(wgt[:], wgt[:], nrec[:].unsqueeze(2).to_broadcast([P, BLK, E]),
                                            ALU.mult).then_inc(wgt_done, 1)
                elif name.startswith("S"):
                    p, s = map(int, name[1:].split("."))
                    bank, full, taken, k = ring_at(name)
                    if s == 0:
                        dve.wait_ge(m_done, PAIRS * j + max(p - 1, 0))
                    dve.wait_ge(full, RING_PER * j + k + 1)
                    nc.vector.tensor_reduce(nmax[:, p % 2, s // 2, s % 2:s % 2 + 1], bank[:], AX.X, ALU.max,
                                            negate=True).then_inc(taken, 1)
                    if s == 2 * BLK - 1:
                        ring_wait(dve, ring_taken, j, f"S{p}.{s - 1}")
                        ring_wait(dve, ring_taken, j, f"S{p}.{s}")
                        m_hi, m_lo = qa[:, :, 2 * p:2 * p + 2, KS], qa[:, :, 2 * p:2 * p + 2, KS + 1]
                        nc.vector.tensor_copy(m_hi.bitcast(F32R), nmax[:, p % 2, :, :]).then_inc(mhi_done, 1)
                        dve.wait_ge(mhi_done, PAIRS * j + p + 1)
                        nc.vector.tensor_tensor(m_lo.bitcast(F32R), nmax[:, p % 2, :, :], m_hi,
                                                ALU.subtract).then_inc(m_done, 1)

            def normalise(i, n):
                dve.wait_ge(misc_full, MISC_PER * i + n + 1)
                parts = misc[:].rearrange("p (b k v) -> p b v k", b=BLK, k=BLK)[:, :, 0:HD + 1, :]
                nc.vector.tensor_reduce(ov[:, n % 2, :, :], parts, AX.X, ALU.add).then_inc(misc_taken, 1)
                dve.wait_ge(misc_taken, MISC_PER * i + n + 1)
                nc.vector.reciprocal(orec[:, n % 2, :], ov[:, n % 2, :, HD]).then_inc(orec_done, 1)
                dve.wait_ge(orec_done, H * i + n + 1)
                nc.vector.tensor_tensor(o_tok[:, :, n * HD:(n + 1) * HD], ov[:, n % 2, :, 0:HD],
                                        orec[:, n % 2, :].unsqueeze(2).to_broadcast([P, BLK, HD]),
                                        ALU.mult).then_inc(norm_done, 1)

            def back(i, u, point):
                if u and point == "turn":
                    normalise(i, 2 * (u - 1))
                    normalise(i, 2 * (u - 1) + 1)

            def tail(i):
                for c in range(DC):
                    dve.wait_ge(oThi_done, DC * i + c + 1)
                    nc.vector.tensor_tensor(oT[:, 1, c, :], misc[:], oT[:, 0, c, :].bitcast(F32),
                                            ALU.subtract).then_inc(misc_taken, 1)
                dve.wait_ge(acc_in, 16 * i + 16)
                for half in range(2):
                    dve.wait_ge(misc_full, MISC_PER * i + H + DC + half + 1)
                    at = slice(2 * half, 2 * half + 2)
                    nc.vector.tensor_tensor(acc[:, at, :], misc[:].rearrange("p (b d) -> p b d", b=2), acc[:, at, :],
                                            ALU.add).then_inc(misc_taken, 1)

            both_phases(dve, back, front, tail)

            def experts(b):
                for c in range(NCH):
                    k = NCH * b + c
                    dve.wait_ge(silu_done, k + 1)
                    dve.wait_ge(up_full, k + 1)
                    dve.wait_ge(hlo_done, NCH * b + max(c - 1, 0))
                    nc.vector.tensor_tensor(hid[:, c % 2, :], up_ps[c % 2], act_g[:, c % 2, :],
                                            ALU.mult).then_inc(gu_done, 1)
                    dve.wait_ge(gu_done, k + 1)
                    dve.wait_ge(wps_full, k + 1)
                    nc.vector.tensor_tensor(hid[:, c % 2, :], hid[:, c % 2, :], wgt_ps[:], ALU.mult).then_inc(hid_done, 1)
                dve.wait_ge(down_used, NCH * b + NCH)
                dve.wait_ge(turn_full, 2 * b)
                nc.vector.tensor_copy(dT[:, 1, :], down_ps[:, 1, :]).then_inc(dT_done, 1)
                dve.wait_ge(acc2_in, 16 * b + 16)
                for half in range(2):
                    dve.wait_ge(turn_full, 2 * b + half + 1)
                    at = slice(2 * half, 2 * half + 2)
                    nc.vector.tensor_tensor(acc2[:, at, :], acc2[:, at, :],
                                            turn_ps[:].rearrange("p (b d) -> p b d", b=2), ALU.add).then_inc(turn_taken, 1)

            experts(0)
            with dve.Fori(1, NB) as b:
                experts(b)

        @block.tensor
        def _(pe):
            def three(dst, stat_hi, stat_lo, mov_hi, mov_lo, first, last):
                pe.matmul(dst, stat_hi, mov_hi, start=first, stop=False)
                pe.matmul(dst, stat_hi, mov_lo, start=False, stop=False)
                return pe.matmul(dst, stat_lo, mov_hi, start=False, stop=last)

            def front(i, j, name):
                if name in ("norm", "rope", "route"):
                    return
                bank, full, taken, k = ring_at(name)
                pe.wait_ge(taken, RING_PER * j + k)
                if name.startswith("xT"):
                    c = int(name[2:])
                    pe.wait_ge(xn_done, BLK * j + BLK)
                    pe.wait_ge(consts_in, 64)
                    for b in range(BLK):
                        mm = pe.transpose(bank[:, b * P:(b + 1) * P], xn[:, b, c * P:(c + 1) * P], identf[:])
                elif name.startswith("proj"):
                    b = int(name[4:])
                    if b == 0:
                        ring_wait(pe, ring_taken, j, "xT1")
                    pe.wait_ge(wa_split, 1)
                    at = slice(b * P, (b + 1) * P)
                    for c in range(DC):
                        mm = three(bank[:, 0:NPROJ], xT[:, 0, c, at], xT[:, 1, c, at], wa_hi[:, c, :], wa_lo[:, c, :],
                                   c == 0, c == DC - 1)
                elif name == "kT":
                    pe.wait_ge(ka_done, j + 1)
                    for b in range(BLK):
                        mm = pe.transpose(bank[:, b * P:(b + 1) * P], ka[:, b, :, :].rearrange("p t s -> p (t s)"), identf[:])
                elif name == "wT":
                    pe.wait_ge(w3_done, j + 1)
                    pe.wait_ge(identb_done, 1)
                    for b in range(BLK):
                        mm = pe.transpose(bank[:].bitcast(BF16)[0:3 * E, b * P:(b + 1) * P], w3[:, b, :], identb[:])
                elif name.startswith("q"):
                    with_max = name.startswith("qm")
                    p = int(name[3:] if with_max else name[2:])
                    if with_max:
                        pe.wait_ge(m_done, PAIRS * j + p + 1)
                    else:
                        pe.wait_ge(qa_done, j + 1)
                    for b in range(BLK):
                        mm = pe.transpose(bank[:, b * P:(b + 1) * P],
                                          qa[:, b, 2 * p:2 * p + 2, :].rearrange("p h s -> p (h s)"), identf[:])
                else:
                    p, s = map(int, name[1:].split("."))
                    qb, lo = s // 2, HS * (s % 2)
                    if s == 0 and (RING[f"qT{p}"] - RING[name]) % 2:
                        ring_wait(pe, ring_taken, j, f"qT{p}")
                    mm = pe.matmul(bank[:], qT[lo:lo + KS, p % 2, qb * P:(qb + 1) * P], kT_new[lo:lo + KS, :],
                                   start=True, stop=True, tile_position=(lo, 0))
                mm.then_inc(full, 1)

            def scores(i, p, kb):
                n = BLK * p + kb
                pe.wait_ge(exp_done, 4 * PAIRS * i + max(n - 1, 0))
                for h in range(2):
                    lo = HS * h
                    mm = pe.matmul(sT[n % 2][:, h, :], kT_cur[lo:lo + KM, kb * P:(kb + 1) * P], qmT[lo:lo + KM, p, :],
                                   start=True, stop=True, tile_position=(lo, 0))
                mm.then_inc(sT_full, 1)

            def probs_v(i, n, kbs):
                if kbs[0] == 0:
                    pe.wait_ge(exp_done, 4 * PAIRS * i + 4 * (n // 2 + 1))
                    pe.wait_ge(pvs_done, H * i + n)
                for kb in kbs:
                    mm = pe.matmul(pv[VW * kb:VW * (kb + 1), :], v_cur[:, kb, :], probs[:, (n // 2) % 2, kb, n % 2, :],
                                   start=True, stop=True, tile_position=(0, VW * kb))
                if kbs[-1] == BLK - 1:
                    mm.then_inc(pv_full, 1)

            def turn(i, n):
                pe.wait_ge(pvs_done, H * i + n + 1)
                pe.wait_ge(misc_taken, MISC_PER * i + n)
                for b in range(BLK):
                    mm = pe.transpose(misc[:, b * P:(b + 1) * P], pvs[:, n % 2, b * P:(b + 1) * P], identf[:])
                mm.then_inc(misc_full, 1)

            def back(i, u, point):
                if u < PAIRS and point == "sT01":
                    if u == 0:
                        pe.wait_ge(kv_cur, 2 * i + 2)
                        pe.wait_ge(ring_taken[0], RING_PER * i + RING_PER)
                        pe.wait_ge(ring_taken[1], RING_PER * i + RING_PER)
                    scores(i, u, 0)
                    scores(i, u, 1)
                if u < PAIRS and point == "sT23":
                    scores(i, u, 2)
                    scores(i, u, 3)
                if u and point[:3] in ("pv0", "pv1"):
                    probs_v(i, 2 * (u - 1) + int(point[2]), (0, 1) if point[3] == "a" else (2, 3))
                if u and point == "turn":
                    turn(i, 2 * (u - 1))
                    turn(i, 2 * (u - 1) + 1)

            def tail(i):
                pe.wait_ge(norm_done, H * i + H)
                for c in range(DC):
                    pe.wait_ge(misc_taken, MISC_PER * i + H + c)
                    for b in range(BLK):
                        mm = pe.transpose(misc[:, b * P:(b + 1) * P], o_tok[:, b, c * P:(c + 1) * P], identf[:])
                    mm.then_inc(misc_full, 1)
                pe.wait_ge(wo_split, 1)
                for half in range(2):
                    pe.wait_ge(misc_taken, MISC_PER * i + H + DC + half)
                    for b in range(2):
                        at = slice((2 * half + b) * P, (2 * half + b + 1) * P)
                        for c in range(DC):
                            mm = three(misc[:, b * D:(b + 1) * D], oT[:, 0, c, at], oT[:, 1, c, at],
                                       wo_hi[:, c, :], wo_lo[:, c, :], c == 0, c == DC - 1)
                    mm.then_inc(misc_full, 1)

            both_phases(pe, back, front, tail)

            def project(b, c, w_hi, w_lo, dst):
                at = slice(c * P, (c + 1) * P)
                for dc in range(DC):
                    mm = three(dst, w_hi[:, dc, at], w_lo[:, dc, at], xT2[:, 0, dc, :], xT2[:, 1, dc, :],
                               dc == 0, dc == DC - 1)
                return mm

            def down(b, c):
                if c == 0:
                    pe.wait_ge(dT_done, 2 * b)
                pe.wait_ge(hlo_done, NCH * b + c + 1)
                pe.wait_ge(lo_done, order["d", c // GC] + 1)
                for dc in range(DC):
                    at = slice(dc * P, (dc + 1) * P)
                    mm = three(down_ps[:, dc, :], d_hi[:, c, at], d_lo[:, c, at], h_hi[:, c % 2, :], h_lo[:, c % 2, :],
                               c == 0, c == NCH - 1)
                mm.then_inc(down_used, 1)

            for bank in range(2):
                pe.wait_ge(ring_taken[bank], RING_PER * NB)
            pe.wait_ge(misc_taken, MISC_PER * NB)
            def experts(b):
                pe.wait_ge(xT2_in, 16 * b + 16)
                for c in range(NCH + 2):
                    if c < NCH:
                        pe.wait_ge(lo_done, order["u", c // GC] + 1)
                        pe.wait_ge(silu_done, NCH * b + max(c - 1, 0))
                        project(b, c, g_hi, g_lo, gate_ps[c % 2][:]).then_inc(gate_full, 1)
                        pe.wait_ge(gu_done, NCH * b + max(c - 1, 0))
                        project(b, c, u_hi, u_lo, up_ps[c % 2]).then_inc(up_full, 1)
                        pe.wait_ge(hid_done, NCH * b + c)
                        pe.matmul(wgt_ps[:], sel_sb[:, c * P:(c + 1) * P], wT3[:, bass.ds(b * T, T)],
                                  start=True, stop=True).then_inc(wps_full, 1)
                    if c >= 2:
                        down(b, c - 2)
                pe.wait_ge(dT_done, 2 * b + 2)
                for half in range(2):
                    pe.wait_ge(turn_taken, 2 * b + half)
                    for k in range(2):
                        at = slice((2 * half + k) * P, (2 * half + k + 1) * P)
                        for dc in range(DC):
                            mm = pe.transpose(turn_ps[:, k * D + dc * P:k * D + (dc + 1) * P], dT[:, dc, at], identf[:])
                    mm.then_inc(turn_full, 1)

            experts(0)
            with pe.Fori(1, NB) as b:
                experts(b)


_INS = ["L0_attn_x", "L0_attn_w_attn", "L0_attn_w_out", "L0_ffn_gate_kernel", "L0_ffn_gate_proj", "L0_ffn_up_proj",
        "L0_ffn_down_proj"]


def _constants():
    pos = np.float32(10000.0) ** ((np.float32(-2.0) * np.arange(0, HD, 2, dtype=np.float32) - np.float32(1.0)) / np.float32(HD))
    angles = np.arange(T, dtype=np.float32)[:, None] * pos[None, :].astype(np.float32)
    c, s = np.cos(angles).astype(np.float32), np.sin(angles).astype(np.float32)

    def tokens_on_partitions(a):
        return np.ascontiguousarray(a.reshape(BLK, P, HD).transpose(1, 0, 2))

    return {
        "cos": tokens_on_partitions(np.concatenate([c, c], 1)),
        "sin": tokens_on_partitions(np.concatenate([-s, s], 1)),
        "ident": np.eye(P, dtype=np.float32),
        "sel": np.tile(np.repeat(np.eye(E, dtype=np.float16), M, axis=1), (3, 1)),
    }


def kernel(**inputs):
    import numpy as _np
    import concourse.bacc as _bacc
    from concourse import mybir as _mybir
    from concourse.bass_utils import run_bass_kernel_spmd as _run

    nc = _bacc.Bacc("TRN2", target_bir_lowering=False, num_devices=1)
    arrays, args = {}, []
    given = {name: _np.ascontiguousarray(inputs[name]) for name in _INS}
    for name, a in {**given, **_constants()}.items():
        arrays[f"in_{name}_dram"] = a
        args.append(nc.dram_tensor(f"in_{name}_dram", a.shape, _mybir.dt.from_np(a.dtype), kind="ExternalInput").ap())
    out = nc.dram_tensor("out_0_dram", (NB, T, D), _mybir.dt.float32, kind="ExternalOutput").ap()
    program(nc, *args, out)
    r = _run(nc, [arrays], core_ids=[0])
    return r.results[0]["out_0_dram"]
```

```python
from contextlib import ExitStack

import numpy as np

import concourse.bass as bass
from concourse import mybir

F32 = mybir.dt.float32
F32R = mybir.dt.float32r
BF16 = mybir.dt.bfloat16
FP16 = mybir.dt.float16
ALU = mybir.AluOpType
ACT = mybir.ActivationFunctionType
AX = mybir.AxisListType

P = 128
NB, T, D = 4, 512, 256
BLK = T // P
DC = D // P
H, HD = 16, 16
HALF = HD // 2
NQK = (H + 1) * HD
NQKV = (H + 2) * HD
E, M, TOPK = 32, 96, 8
NPROJ = NQKV + E
HID = E * M
NCH = HID // P
GE = 4
GH = GE * M
GC = GH // P
NG = E // GE
HS = 64
KS = 3 * HD
KM = KS + 2
PAIRS = H // 2
VW = 32
SCALE = HD ** -0.5
EPS = 1e-5

RING_OFF = ("norm", "rope", "split0", "split1", "route")


def prologue_steps():
    steps = ["norm", "xT0", "xT1", "proj0", "proj1", "proj2", "proj3", "rope", "split0", "kT", "qT0", "qT1"]
    steps += [f"S0.{s}" for s in range(2 * BLK)] + ["split1", "qT2", "route"]
    steps += [f"S1.{s}" for s in range(2 * BLK)]
    steps.insert(steps.index("S1.4"), "qmT0")
    return [(0, name) for name in steps + ["wT"]]


PREPARE = {(0, 0): ["norm"], (1, 2): ["xT0", "xT1"], (1, 4): ["proj0", "proj1"], (2, 2): ["proj2", "proj3"],
           (2, 3): ["rope"], (3, 2): ["route"], (4, 1): ["split0"], (4, 3): ["wT"], (5, 4): ["kT"],
           (6, 4): ["split1"]}
POINTS = 5


def window_plan(more):
    def pair(u):
        return u // PAIRS, u % PAIRS

    plan = {}
    for u in range(PAIRS):
        (ds, ps), (dq, pq), (dm, pm) = pair(u + 2), pair(u + 3), pair(u + 1)
        s = [(ds, f"S{ps}.{n}") for n in range(2 * BLK)]
        at = [s[0:2], [(dm, f"qmT{pm}"), s[2]], s[3:5], s[5:7], [s[7]]]
        for point in range(POINTS):
            steps = at[point] + [(1, name) for name in PREPARE.get((u, point), [])]
            if point == POINTS - 1:
                steps.append((dq, f"qT{pq}"))
            plan[u, point] = [(ahead, name) for ahead, name in steps if more or not ahead]
    return plan


def ring_order(steps):
    return {step: n for n, step in enumerate(st for st in steps if st[1] not in RING_OFF)}


PROLOGUE = prologue_steps()
PLAN, LAST_PLAN = window_plan(True), window_plan(False)
ORDER0 = ring_order(PROLOGUE)
ORDER = ring_order(step for steps in PLAN.values() for step in steps)
LAST_ORDER = ring_order(step for steps in LAST_PLAN.values() for step in steps)
assert len(ORDER0) % 2 == 0 and len(ORDER) % 2 == 0 and len(LAST_ORDER) % 2 == 0
RING0, RING_PER, RING_LAST = len(ORDER0) // 2, len(ORDER) // 2, len(LAST_ORDER) // 2

MISC = {name: n for n, name in enumerate("Tp6 Tp7 O0 O1 T0 P0 T1 P1 T2 T3 T4 T5".split())}
MISC_FIRST = {f"T{p}": p for p in range(PAIRS - 2)}
LATE = {1: ("O0", "O1"), 2: ("P0",), 3: ("P1",)}
MISC_END = {name: n for n, name in enumerate("Tp6 Tp7 O0 O1 P0 P1".split())}


def program(nc, x, w_attn, w_out, gate_kernel, gate_proj, up_proj, down_proj, cos, sin, ident, sel, out):
    down_rows = down_proj.rearrange("e m d -> (e m) d")
    xT_dram = nc.dram_tensor("xT_spill", (NB, P, 2 * DC * T), F32, kind="Internal").ap()
    acc_dram = nc.dram_tensor("acc_spill", (NB, P, BLK * D), F32, kind="Internal").ap()

    with ExitStack() as ctx:
        def sb(name, shape, dt=F32, where=ctx):
            return where.enter_context(nc.sbuf_tensor(name, shape, dt))

        def psum(name, shape):
            return ctx.enter_context(nc.psum_tensor(name, shape, F32))

        def sems(names):
            return [ctx.enter_context(nc.semaphore(name)) for name in names.split()]

        identf = sb("identf", [P, P])
        identb = sb("identb", [P, P], BF16)
        sel_sb = sb("sel_sb", [3 * E, HID], FP16)
        wT3 = sb("wT3", [3 * E, NB * T], BF16)
        stage = sb("stage", [P, 3, DC * GH])
        w_raw = stage[:].rearrange("p s n -> p (s n)")[:, 0:DC * (NPROJ + D)].rearrange("p (c n) -> p c n", c=DC)
        g_hi, g_lo = sb("g_hi", [P, DC, HID], F32R), sb("g_lo", [P, DC, HID], F32R)

        ph1 = ExitStack()
        cs = sb("cs", [P, 2, BLK, HD], where=ph1)
        wa_hi, wa_lo = (sb(n, [P, DC, NPROJ], F32R, ph1) for n in ("wa_hi", "wa_lo"))
        wo_hi, wo_lo = (sb(n, [P, DC, D], F32R, ph1) for n in ("wo_hi", "wo_lo"))
        xs = sb("xs", [P, BLK, D], where=ph1)
        xn = sb("xn", [P, BLK, D], where=ph1)
        bn = sb("bn", [P, BLK, 6], where=ph1)
        mv = sb("mv", [P, BLK, 2], where=ph1)
        veps = sb("veps", [P, BLK], where=ph1)
        rstd = sb("rstd", [P, BLK], where=ph1)
        mhalf = sb("mhalf", [P, BLK], where=ph1)
        xT = sb("xT", [P, 2, DC, T], F32R, ph1)
        qkv = sb("qkv", [P, BLK, NPROJ], where=ph1)
        rot_c = sb("rot_c", [P, BLK, NQK], where=ph1)
        rot_s = sb("rot_s", [P, BLK, NQK], where=ph1)
        qa = sb("qa", [P, BLK, H, HS], where=ph1)
        ka = sb("ka", [P, BLK, 2, HS], where=ph1)
        kT_new = sb("kT_new", [P, T], F32R, ph1)
        kT_cur = sb("kT_cur", [P, T], F32R, ph1)
        v_new = sb("v_new", [P, BLK, VW], where=ph1)
        v_cur = sb("v_cur", [P, BLK, VW], where=ph1)
        qT = sb("qT", [P, 2, T], F32R, ph1)
        qmT = sb("qmT", [P, 2, T], F32R, ph1)
        nmax = sb("nmax", [P, 2, BLK, 2], where=ph1)
        lmax = sb("lmax", [P, BLK], where=ph1)
        ex = sb("ex", [P, BLK, E], where=ph1)
        top8 = sb("top8", [P, BLK, TOPK], where=ph1)
        rest = sb("rest", [P, BLK, E], where=ph1)
        nsum = sb("nsum", [P, BLK], where=ph1)
        nrec = sb("nrec", [P, BLK], where=ph1)
        wgt = sb("wgt", [P, BLK, E], where=ph1)
        w3 = sb("w3", [P, BLK, 3 * E], BF16, ph1)
        probs = sb("probs", [P, 2, BLK, 2, T], where=ph1)
        pvs = sb("pvs", [P, 2, T], where=ph1)
        ov = sb("ov", [P, 2, BLK, 2, HD + 1], where=ph1)
        orec = sb("orec", [P, 2, BLK, 2], where=ph1)
        o_tok = sb("o_tok", [P, BLK, D], where=ph1)
        oT = sb("oT", [P, 2, DC, T], F32R, ph1)
        acc = sb("acc", [P, BLK, D], where=ph1)
        ph1.close()

        u_hi, u_lo = sb("u_hi", [P, DC, HID], F32R), sb("u_lo", [P, DC, HID], F32R)
        d_hi, d_lo = sb("d_hi", [P, NCH, D], F32R), sb("d_lo", [P, NCH, D], F32R)
        xT2 = sb("xT2", [P, 2, DC, T], F32R)
        act_g = sb("act_g", [P, 2, T])
        hid = sb("hid", [P, 2, T])
        h_hi, h_lo = sb("h_hi", [P, 2, T], F32R), sb("h_lo", [P, 2, T], F32R)
        dT = sb("dT", [P, DC, T])
        acc2 = sb("acc2", [P, BLK, D])

        ring = [psum(f"ring{i}", [P, T]) for i in range(2)]
        sT = [psum(f"sT{i}", [P, 2, T]) for i in range(2)]
        pv, misc = psum("pv", [P, T]), psum("misc", [P, T])
        gate_ps, up_ps, down_ps, wgt_ps, turn_ps = ring, (sT[0][:, 0, :], sT[0][:, 1, :]), sT[1], pv, misc

        consts_in, w_in, wa_hi_done, wo_hi_done, wa_split, wo_split, fixed, identb_done = sems(
            "consts_in w_in wa_hi_done wo_hi_done wa_split wo_split fixed identb_done")
        (waited_apart,) = sems("waited_apart")
        x_in, bn_done, mv_done, veps_done, rstd_done, xn_done, xThi_done, xT_out = sems(
            "x_in bn_done mv_done veps_done rstd_done xn_done xThi_done xT_out")
        ring_full, ring_taken = sems("ring_full0 ring_full1"), sems("ring_taken0 ring_taken1")
        rotc_done, rots_done, rot_done, qhi_done, qa_done, khi_done, ka_done, v_done, kT_cur_done, v_cur_done = sems(
            "rotc_done rots_done rot_done qhi_done qa_done khi_done ka_done v_done kT_cur_done v_cur_done")
        lmax_done, lsub_done, ex_done, top8_done, rest_done, nsum_done, nrec_done, selneg_done, wgt_done = sems(
            "lmax_done lsub_done ex_done top8_done rest_done nsum_done nrec_done selneg_done wgt_done")
        w3a_done, w3r_done, w3b_done, w3_done, mhi_done, m_done = sems(
            "w3a_done w3r_done w3b_done w3_done mhi_done m_done")
        (ov_done,) = sems("ov_done")
        sT_full, exp_done, pv_full, pvs_done, misc_full, misc_taken, orec_done, norm_done, oThi_done = sems(
            "sT_full exp_done pv_full pvs_done misc_full misc_taken orec_done norm_done oThi_done")
        acc_in, acc_out = sems("acc_in acc_out")
        stage_in = sems("stage_in0 stage_in1 stage_in2")
        hi_done, lo_done = sems("hi_done lo_done")
        xT2_in, acc2_in, gate_full, up_full, wps_full, silu_done, gu_done, hid_done, hhi_done, hlo_done = sems(
            "xT2_in acc2_in gate_full up_full wps_full silu_done gu_done hid_done hhi_done hlo_done")
        down_used, dT_done, turn_full, turn_taken, out_done = sems(
            "down_used dT_done turn_full turn_taken out_done")

        def ring_use(win, ahead, name):
            table, before, before_last = win
            if (ahead, name) in table:
                n = table[ahead, name]
                return n % 2, before + n // 2
            if before_last is None:
                n = ORDER0[0, name]
                return n % 2, n // 2
            n = ORDER[ahead + 1, name]
            return n % 2, before_last + n // 2

        WIN0 = (ORDER0, 0, None)

        def win_at(b, table=ORDER):
            if isinstance(b, int) and b == 0:
                return table, RING0, None
            return table, RING_PER * b + RING0, RING_PER * b + (RING0 - RING_PER)

        def ring_wait(eng, which, win, ahead, name):
            bank, n = ring_use(win, ahead, name)
            eng.wait_ge(which[bank], n + 1)

        def windows(eng, slot, front):
            def window(b, plan, win):
                for u in range(PAIRS):
                    for point in range(POINTS):
                        slot(win, b, u, point)
                        for ahead, name in plan[u, point]:
                            front(win, b + ahead, ahead, name)

            for ahead, name in PROLOGUE:
                front(WIN0, 0, ahead, name)
            slot(None, 0, None, None)
            window(0, PLAN, win_at(0))
            with eng.Fori(1, NB - 1) as b:
                window(b, PLAN, win_at(b))
            window(NB - 1, LAST_PLAN, win_at(NB - 1, LAST_ORDER))
            slot(None, NB, None, None)

        def misc_use(b, name):
            if isinstance(b, int) and b == 0:
                return MISC_FIRST[name]
            if isinstance(b, int) and b == NB:
                return len(MISC) * NB - 6 + MISC_END[name]
            return len(MISC) * b - 6 + MISC[name]

        def wait_apart(eng, semaphore, value):
            eng.wait_ge(semaphore, value)
            eng.sem_inc(waited_apart, 1)

        groups = [("g", g) for g in range(NG)]
        for g in range(NG):
            groups += [("u", g), ("d", g)]
        order = {key: n for n, key in enumerate(groups)}

        W_HILO = {"g": (g_hi, g_lo), "u": (u_hi, u_lo), "d": (d_hi, d_lo)}

        def group_at(n):
            kind, g = groups[n]
            raw = stage[:, n % 3, :].rearrange("p (r d) -> p r d", r=GC if kind == "d" else DC)
            if kind == "d":
                return [raw] + [w[:, g * GC:(g + 1) * GC, :] for w in W_HILO[kind]]
            return [raw] + [w[:, :, g * GH:(g + 1) * GH] for w in W_HILO[kind]]

        def rotated(half):
            heads = slice(half * H // 2, (half + 1) * H // 2)
            return rot_c[:].rearrange("p b (h d) -> p b h d", d=HD)[:, :, heads, :], qa[:, :, heads, :]

        block = ctx.enter_context(nc.Block())

        @block.sync
        def _(sp):
            def tok(a, b):
                return a[bass.ds(b, 1), :, :].rearrange("o (b p) d -> p (o b) d", p=P)

            def row(a, b):
                return a[bass.ds(b, 1), :, :].rearrange("o p n -> p (o n)")

            def load_x(j):
                sp.wait_ge(xn_done, BLK * j)
                sp.dma_start(xs[:], tok(x, j)).then_inc(x_in, 16)

            def load_group(n):
                kind, g = groups[n]
                if n >= 3:
                    sp.wait_ge(lo_done, n - 2)
                slot = stage[:, n % 3, :]
                if kind == "d":
                    to = slot.rearrange("p (r d) -> p r d", r=GC)
                    rows = down_rows[g * GH:(g + 1) * GH, :].rearrange("(r p) d -> p r d", p=P)
                    sp.dma_start(to[:, 0:2, :], rows[:, 0:2, :]).then_inc(stage_in[n % 3], 16)
                    sp.dma_start(to[:, 2:GC, :], rows[:, 2:GC, :]).then_inc(stage_in[n % 3], 16)
                else:
                    w = gate_proj if kind == "g" else up_proj
                    for c in range(DC):
                        sp.dma_start(slot[:, c * GH:(c + 1) * GH].rearrange("p (e m) -> p e m", e=GE),
                                     w[g * GE:(g + 1) * GE, c * P:(c + 1) * P, :].rearrange("e p m -> p e m")
                                     ).then_inc(stage_in[n % 3], 16)

            def load_residual(i):
                sp.wait_ge(acc_out, 16 * i)
                sp.dma_start(acc[:], tok(x, i)).then_inc(acc_in, 16)

            def spill_xT(win, j, ahead):
                ring_wait(sp, ring_taken, win, ahead, "xT0")
                ring_wait(sp, ring_taken, win, ahead, "xT1")
                sp.dma_start(row(xT_dram, j), xT[:].rearrange("p a c t -> p (a c t)").bitcast(F32)).then_inc(xT_out, 16)

            def spill_acc(i):
                sp.wait_ge(misc_taken, misc_use(i + 1, "P1") + 1)
                sp.dma_start(row(acc_dram, i), acc[:].rearrange("p b d -> p (b d)")).then_inc(acc_out, 16)

            sp.dma_start(xs[:], tok(x, 0)).then_inc(x_in, 16)
            sp.dma_start(w_raw[:, :, 0:NQKV], w_attn.rearrange("(c p) n -> p c n", p=P)).then_inc(w_in, 16)
            sp.dma_start(w_raw[:, :, NQKV:NPROJ], gate_kernel.rearrange("(c p) n -> p c n", p=P)).then_inc(w_in, 16)
            sp.dma_start(identf[:], ident).then_inc(consts_in, 16)
            sp.dma_start(cs[:, 0, :, :], cos).then_inc(consts_in, 16)
            sp.dma_start(cs[:, 1, :, :], sin).then_inc(consts_in, 16)
            sp.dma_start(w_raw[:, :, NPROJ:NPROJ + D], w_out.rearrange("(c p) n -> p c n", p=P)).then_inc(w_in, 16)
            sp.dma_start(sel_sb[:], sel).then_inc(consts_in, 16)
            sp.dma_start(acc[:], tok(x, 0)).then_inc(acc_in, 16)
            load_x(1)
            spill_xT(WIN0, 0, 0)
            sp.wait_ge(wo_split, 1)
            for n in range(4):
                load_group(n)
            load_x(2)
            spill_xT(win_at(0), 1, 1)
            for n in range(4, NG):
                load_group(n)
            with sp.Fori(1, NB - 2) as b:
                load_x(b + 2)
                spill_xT(win_at(b), b + 1, 1)
                spill_acc(b - 1)
                load_residual(b)
            spill_xT(win_at(NB - 2), NB - 1, 1)
            spill_acc(NB - 3)
            load_residual(NB - 2)
            for n in range(NG, NG + 3):
                load_group(n)
            spill_acc(NB - 2)
            load_residual(NB - 1)
            spill_acc(NB - 1)

            def load_batch(b):
                sp.wait_ge(up_full, NCH * b)
                sp.dma_start(xT2[:].rearrange("p a c t -> p (a c t)").bitcast(F32), row(xT_dram, b)).then_inc(xT2_in, 16)

            def load_acc(b):
                sp.wait_ge(out_done, 32 * b)
                sp.dma_start(acc2[:].rearrange("p b d -> p (b d)"), row(acc_dram, b)).then_inc(acc2_in, 16)

            def store(b):
                for half in range(2):
                    sp.wait_ge(turn_taken, 2 * b + half + 1)
                    sp.dma_start(tok(out, b)[:, 2 * half:2 * half + 2, :],
                                 acc2[:, 2 * half:2 * half + 2, :]).then_inc(out_done, 16)

            sp.wait_ge(xT_out, 16 * NB)
            sp.wait_ge(acc_out, 16 * NB)
            load_batch(0)
            for n in range(NG + 3, len(groups)):
                load_group(n)
                if n == NG + 5:
                    sp.dma_start(acc2[:].rearrange("p b d -> p (b d)"), row(acc_dram, 0)).then_inc(acc2_in, 16)
            with sp.Fori(0, NB - 1) as b:
                load_batch(b + 1)
                store(b)
                load_acc(b + 1)
            store(NB - 1)
            sp.wait_ge(out_done, 32 * NB)

        @block.gpsimd
        def _(pool):
            nc.gpsimd.memset(mhalf[:], -0.5).then_inc(fixed, 1)
            nc.gpsimd.memset(qa[:].rearrange("p b h s -> p (b h) s")[:, :, KS:HS], 0.0).then_inc(fixed, 1)
            kav = ka[:].rearrange("p b t s -> p (b t) s")
            nc.gpsimd.memset(kav[:, :, KS:KM], 1.0).then_inc(fixed, 1)
            nc.gpsimd.memset(kav[:, :, KM:HS], 0.0).then_inc(fixed, 1)
            nc.gpsimd.memset(v_new[:, :, HD:HD + 1], 1.0).then_inc(fixed, 1)
            nc.gpsimd.memset(v_new[:, :, HD + 1:VW], 0.0).then_inc(fixed, 1)

            def norm(j):
                wait_apart(pool, mv_done, BLK * j + BLK)
                nc.gpsimd.tensor_scalar(veps[:], mv[:, :, 1], EPS, None, ALU.add).then_inc(veps_done, 1)
                pool.wait_ge(veps_done, j + 1)
                pool.wait_ge(xn_done, BLK * j)
                nc.gpsimd.tensor_tensor(rstd[:], veps[:], mhalf[:], ALU.pow).then_inc(rstd_done, 1)

            def rope(win, j, ahead):
                ring_wait(pool, ring_taken, win, ahead, "proj2")
                ring_wait(pool, ring_taken, win, ahead, "proj3")
                pool.wait_ge(qhi_done, 4 * j)
                pool.wait_ge(qa_done, 2 * j)
                xv = qkv[:, :, 0:NQK].rearrange("p b (h d) -> p b h d", d=HD)
                rc = rot_c[:].rearrange("p b (h d) -> p b h d", d=HD)
                rs = rot_s[:].rearrange("p b (h d) -> p b h d", d=HD)

                def table(which, lo, hi):
                    return cs[:, which, :, lo:hi].unsqueeze(2).to_broadcast([P, BLK, H + 1, hi - lo])

                nc.gpsimd.tensor_tensor(rc, xv, table(0, 0, HD), ALU.mult).then_inc(rotc_done, 1)
                nc.gpsimd.tensor_tensor(rs[:, :, :, 0:HALF], xv[:, :, :, HALF:HD], table(1, 0, HALF),
                                        ALU.mult).then_inc(rots_done, 1)
                nc.gpsimd.tensor_tensor(rs[:, :, :, HALF:HD], xv[:, :, :, 0:HALF], table(1, HALF, HD),
                                        ALU.mult).then_inc(rots_done, 1)
                pool.wait_ge(rotc_done, j + 1)
                pool.wait_ge(rots_done, 2 * j + 2)
                nc.gpsimd.tensor_tensor(rot_c[:], rot_c[:], rot_s[:], ALU.add).then_inc(rot_done, 1)
                k = rc[:, :, H, :].unsqueeze(2).to_broadcast([P, BLK, 2, HD])
                wait_apart(pool, rot_done, j + 1)
                nc.gpsimd.tensor_copy(ka[:, :, :, 0:HD].bitcast(F32R), k).then_inc(khi_done, 1)
                nc.gpsimd.tensor_copy(ka[:, :, :, 2 * HD:3 * HD].bitcast(F32R), k).then_inc(khi_done, 1)
                pool.wait_ge(khi_done, 2 * j + 2)
                nc.gpsimd.tensor_tensor(ka[:, :, :, HD:2 * HD].bitcast(F32R), k, ka[:, :, :, 0:HD],
                                        ALU.subtract).then_inc(ka_done, 1)

            def split_q(j, half):
                q, parts = rotated(half)
                pool.wait_ge(qhi_done, 4 * j + 2 * half + 2)
                nc.gpsimd.tensor_tensor(parts[:, :, :, 2 * HD:3 * HD].bitcast(F32R), q, parts[:, :, :, 0:HD],
                                        ALU.subtract).then_inc(qa_done, 1)

            def route(j):
                wait_apart(pool, wgt_done, j + 1)
                nc.gpsimd.tensor_copy(w3[:, :, 0:E], wgt[:]).then_inc(w3a_done, 1)
                pool.wait_ge(w3a_done, j + 1)
                nc.gpsimd.tensor_tensor(ex[:], wgt[:], w3[:, :, 0:E], ALU.subtract).then_inc(w3r_done, 1)
                wait_apart(pool, w3r_done, j + 1)
                nc.gpsimd.tensor_copy(w3[:, :, E:2 * E], ex[:]).then_inc(w3b_done, 1)
                pool.wait_ge(w3b_done, j + 1)
                nc.gpsimd.tensor_tensor(w3[:, :, 2 * E:3 * E], ex[:], w3[:, :, E:2 * E], ALU.subtract).then_inc(w3_done, 1)

            def split_group(n):
                raw, hi, lo = group_at(n)
                pool.wait_ge(hi_done, n + 1)
                nc.gpsimd.tensor_tensor(lo, raw, hi.bitcast(F32), ALU.subtract).then_inc(lo_done, 1)

            pool.wait_ge(w_in, 48)
            nc.gpsimd.tensor_copy(wa_hi[:], w_raw[:, :, 0:NPROJ]).then_inc(wa_hi_done, 1)
            norm(0)
            pool.wait_ge(wa_hi_done, 1)
            nc.gpsimd.tensor_tensor(wa_lo[:], w_raw[:, :, 0:NPROJ], wa_hi[:].bitcast(F32), ALU.subtract).then_inc(wa_split, 1)
            rope(WIN0, 0, 0)
            split_q(0, 0)
            split_q(0, 1)
            nc.gpsimd.tensor_copy(wo_hi[:], w_raw[:, :, NPROJ:NPROJ + D]).then_inc(wo_hi_done, 1)
            pool.wait_ge(wo_hi_done, 1)
            nc.gpsimd.tensor_tensor(wo_lo[:], w_raw[:, :, NPROJ:NPROJ + D], wo_hi[:].bitcast(F32), ALU.subtract).then_inc(wo_split, 1)
            route(0)
            norm(1)
            split_group(0)
            split_group(1)
            rope(win_at(0), 1, 1)
            split_group(2)
            route(1)
            split_group(3)
            split_q(1, 0)
            for n in range(4, 6):
                split_group(n)
            split_q(1, 1)
            for n in range(6, NG):
                split_group(n)
            with pool.Fori(1, NB - 1) as b:
                norm(b + 1)
                rope(win_at(b), b + 1, 1)
                route(b + 1)
                split_q(b + 1, 0)
                split_q(b + 1, 1)

            def hidden_lo(b, c):
                pool.wait_ge(hhi_done, NCH * b + c + 1)
                pool.wait_ge(down_used, NCH * b + max(c - 1, 0))
                nc.gpsimd.tensor_tensor(h_lo[:, c % 2, :], hid[:, c % 2, :], h_hi[:, c % 2, :].bitcast(F32),
                                        ALU.subtract).then_inc(hlo_done, 1)

            pool.wait_ge(acc_out, 16 * NB)
            pool.wait_ge(xT_out, 16 * NB)
            split_group(order["u", 0])
            split_group(order["d", 0])
            for c in range(NCH):
                hidden_lo(0, c)
                if c % GC < 2 and c // GC + 1 < NG:
                    split_group(order["ud"[c % GC], c // GC + 1])
            with pool.Fori(1, NB) as b:
                for c in range(NCH):
                    hidden_lo(b, c)

        @block.scalar
        def _(act):
            def take(win, ahead, name, dst, src=None):
                bank, n = ring_use(win, ahead, name)
                act.wait_ge(ring_full[bank], n + 1)
                nc.scalar.activation(dst, ring[bank][:] if src is None else src(ring[bank]), ACT.Copy
                                     ).then_inc(ring_taken[bank], 1)

            def front(win, j, ahead, name):
                if name.startswith("xT"):
                    c = int(name[2:])
                    bank, n = ring_use(win, ahead, name)
                    act.wait_ge(ring_full[bank], n + 1)
                    act.wait_ge(xT_out, 16 * j)
                    nc.scalar.activation(xT[:, 0, c, :], ring[bank][:], ACT.Copy).then_inc(xThi_done, 1)
                elif name.startswith("proj"):
                    b = int(name[4:])
                    if b == 0:
                        act.wait_ge(rot_done, j)
                        act.wait_ge(lsub_done, j)
                        act.wait_ge(v_done, j)
                    take(win, ahead, name, qkv[:, b, :], lambda bank: bank[:, 0:NPROJ])
                elif name == "rope":
                    ring_wait(act, ring_taken, win, ahead, "proj2")
                    ring_wait(act, ring_taken, win, ahead, "proj3")
                    act.wait_ge(v_cur_done, j)
                    act.wait_ge(fixed, 6)
                    nc.scalar.activation(v_new[:, :, 0:HD], qkv[:, :, NQK:NQKV], ACT.Copy).then_inc(v_done, 1)
                elif name.startswith("split"):
                    half = int(name[5:])
                    q, parts = rotated(half)
                    act.wait_ge(rot_done, j + 1)
                    if ahead:
                        ring_wait(act, ring_full, win, 0, f"qmT{(half + 1) * PAIRS // 2 - 1}")
                    for k in range(2):
                        nc.scalar.activation(parts[:, :, :, k * HD:(k + 1) * HD].bitcast(F32R), q, ACT.Copy
                                             ).then_inc(qhi_done, 1)
                elif name == "route":
                    act.wait_ge(lsub_done, j + 1)
                    nc.scalar.activation(ex[:], ex[:], ACT.Exp).then_inc(ex_done, 1)
                elif name == "kT":
                    act.wait_ge(kT_cur_done, j)
                    take(win, ahead, name, kT_new[:])
                elif name == "wT":
                    take(win, ahead, name, wT3[:, bass.ds(j * T, T)], lambda bank: bank[0:3 * E, 0:T // 2].bitcast(BF16))
                elif name.startswith("qT"):
                    take(win, ahead, name, qT[:, int(name[2:]) % 2, :])
                elif name.startswith("qmT"):
                    take(win, ahead, name, qmT[:, int(name[3:]) % 2, :])

            def exp(b, u, kb):
                n = BLK * u + kb
                act.wait_ge(sT_full, BLK * PAIRS * b + n + 1)
                if kb == 0:
                    act.wait_ge(pv_full, max(u - 1, 0) if isinstance(b, int) and b == 0 else
                                PAIRS * b + u - 1)
                nc.scalar.activation(probs[:, u % 2, kb, :, :], sT[n % 2][:], ACT.Exp, scale=SCALE).then_inc(exp_done, 1)

            def take_pv(b, p):
                act.wait_ge(pv_full, PAIRS * b + p + 1)
                nc.scalar.activation(pvs[:, p % 2, :], pv[:], ACT.Copy).then_inc(pvs_done, 1)

            def take_v(b):
                if isinstance(b, int) and b == 0:
                    act.wait_ge(v_done, 1)
                nc.scalar.activation(v_cur[:], v_new[:], ACT.Copy).then_inc(v_cur_done, 1)

            def late(b, name):
                if name in ("O0", "O1"):
                    act.wait_ge(misc_full, misc_use(b, name) + 1)
                    nc.scalar.activation(oT[:, 0, int(name[1]), :], misc[:], ACT.Copy).then_inc(oThi_done, 1)

            def slot(win, b, u, point):
                first = isinstance(b, int) and b == 0
                if u is None:
                    if first:
                        take_v(0)
                    else:
                        take_pv(NB - 1, PAIRS - 1)
                        late(b, "O0")
                        late(b, "O1")
                    return
                if point == 0:
                    exp(b, u, 0)
                    exp(b, u, 1)
                elif point == 2:
                    exp(b, u, 2)
                    exp(b, u, 3)
                elif point == 3 and not (first and u == 0):
                    take_pv(b if u else b - 1, (u - 1) % PAIRS)
                    if u == 0:
                        take_v(b)
                elif point == 4:
                    if u == 1 and not first:
                        late(b, "O0")
                        late(b, "O1")
                    if first:
                        split_group(u)

            def split_group(n):
                raw, hi, lo = group_at(n)
                act.wait_ge(stage_in[n % 3], 32 * (n // 3 + 1))
                nc.scalar.activation(hi, raw, ACT.Copy).then_inc(hi_done, 1)

            act.wait_ge(consts_in, 64)
            nc.scalar.activation(identb[:], identf[:], ACT.Copy).then_inc(identb_done, 1)
            windows(act, slot, front)

            def silu(b, c):
                act.wait_ge(gate_full, NCH * b + c + 1)
                act.wait_ge(gu_done, NCH * b + max(c - 1, 0))
                nc.scalar.activation(act_g[:, c % 2, :], gate_ps[c % 2][:], ACT.Silu).then_inc(silu_done, 1)

            def hidden_hi(b, c):
                act.wait_ge(hid_done, NCH * b + c + 1)
                act.wait_ge(down_used, NCH * b + max(c - 1, 0))
                nc.scalar.activation(h_hi[:, c % 2, :], hid[:, c % 2, :], ACT.Copy).then_inc(hhi_done, 1)

            def experts(b, split=False):
                for c in range(NCH + 1):
                    if c < NCH:
                        silu(b, c)
                    if c:
                        hidden_hi(b, c - 1)
                        if split and (c - 1) % GC < 2 and (c - 1) // GC + 1 < NG:
                            split_group(order["ud"[(c - 1) % GC], (c - 1) // GC + 1])
                act.wait_ge(down_used, NCH * b + NCH)
                act.wait_ge(turn_full, 2 * b)
                nc.scalar.activation(dT[:, 0, :], down_ps[:, 0, :], ACT.Copy).then_inc(dT_done, 1)

            act.wait_ge(acc_out, 16 * NB)
            act.wait_ge(xT_out, 16 * NB)
            split_group(order["u", 0])
            split_group(order["d", 0])
            experts(0, split=True)
            with act.Fori(1, NB) as b:
                experts(b)

        @block.vector
        def _(dve):
            def front(win, j, ahead, name):
                if name == "norm":
                    dve.wait_ge(x_in, 16 * j + 16)
                    for b in range(BLK):
                        nc.vector.bn_stats(bn[:, b, :], xs[:, b, :]).then_inc(bn_done, 1)
                    dve.wait_ge(xn_done, BLK * j)
                    wait_apart(dve, bn_done, BLK * j + BLK)
                    for b in range(BLK):
                        nc.vector.bn_aggr(mv[:, b, :], bn[:, b, :]).then_inc(mv_done, 1)
                    dve.wait_ge(rstd_done, j + 1)
                    for b in range(BLK):
                        nc.vector.tensor_scalar(xn[:, b, :], xs[:, b, :], mv[:, b, 0:1], rstd[:, b:b + 1],
                                                ALU.subtract, ALU.mult).then_inc(xn_done, 1)
                elif name.startswith("xT"):
                    c = int(name[2:])
                    bank, n = ring_use(win, ahead, name)
                    dve.wait_ge(xThi_done, DC * j + c + 1)
                    nc.vector.tensor_tensor(xT[:, 1, c, :], ring[bank][:], xT[:, 0, c, :].bitcast(F32),
                                            ALU.subtract).then_inc(ring_taken[bank], 1)
                elif name == "route":
                    logits = qkv[:, :, NQKV:NPROJ]
                    ring_wait(dve, ring_taken, win, ahead, "proj2")
                    ring_wait(dve, ring_taken, win, ahead, "proj3")
                    dve.wait_ge(w3_done, j)
                    nc.vector.tensor_reduce(lmax[:], logits, AX.X, ALU.max).then_inc(lmax_done, 1)
                    dve.wait_ge(lmax_done, j + 1)
                    nc.vector.tensor_tensor(ex[:], logits, lmax[:].unsqueeze(2).to_broadcast([P, BLK, E]),
                                            ALU.subtract).then_inc(lsub_done, 1)
                    wait_apart(dve, ex_done, j + 1)
                    for b in range(BLK):
                        nc.vector.max(top8[:, b, :], ex[:, b, :]).then_inc(top8_done, 1)
                    wait_apart(dve, top8_done, BLK * j + BLK)
                    for b in range(BLK):
                        nc.vector.match_replace(out=rest[:, b, :], in_to_replace=top8[:, b, :], in_values=ex[:, b, :],
                                                imm_value=-1.0).then_inc(rest_done, 1)
                    nc.vector.tensor_reduce(nsum[:], top8[:], AX.X, ALU.add, negate=True).then_inc(nsum_done, 1)
                    dve.wait_ge(nsum_done, j + 1)
                    nc.vector.reciprocal(nrec[:], nsum[:]).then_inc(nrec_done, 1)
                    dve.wait_ge(rest_done, BLK * j + BLK)
                    nc.vector.scalar_tensor_tensor(out=wgt[:], in0=rest[:], scalar=0.0, in1=ex[:], op0=ALU.max,
                                                   op1=ALU.subtract).then_inc(selneg_done, 1)
                    dve.wait_ge(nrec_done, j + 1)
                    dve.wait_ge(selneg_done, j + 1)
                    nc.vector.tensor_tensor(wgt[:], wgt[:], nrec[:].unsqueeze(2).to_broadcast([P, BLK, E]),
                                            ALU.mult).then_inc(wgt_done, 1)
                elif name.startswith("S"):
                    p, s = map(int, name[1:].split("."))
                    bank, n = ring_use(win, ahead, name)
                    if s == 0 and not (isinstance(j, int) and PAIRS * j + p < 2):
                        dve.wait_ge(m_done, PAIRS * j + p - 1)
                    dve.wait_ge(ring_full[bank], n + 1)
                    nc.vector.tensor_reduce(nmax[:, p % 2, s // 2, s % 2:s % 2 + 1], ring[bank][:], AX.X, ALU.max,
                                            negate=True).then_inc(ring_taken[bank], 1)
                    if s == 2 * BLK - 1:
                        ring_wait(dve, ring_taken, win, ahead, f"S{p}.{s - 1}")
                        ring_wait(dve, ring_taken, win, ahead, f"S{p}.{s}")
                        m_hi, m_lo = qa[:, :, 2 * p:2 * p + 2, KS], qa[:, :, 2 * p:2 * p + 2, KS + 1]
                        nc.vector.tensor_copy(m_hi.bitcast(F32R), nmax[:, p % 2, :, :]).then_inc(mhi_done, 1)
                        dve.wait_ge(mhi_done, PAIRS * j + p + 1)
                        nc.vector.tensor_tensor(m_lo.bitcast(F32R), nmax[:, p % 2, :, :], m_hi,
                                                ALU.subtract).then_inc(m_done, 1)

            def normalise(w, name, b, p):
                dve.wait_ge(misc_full, misc_use(w, name) + 1)
                sums = misc[:].rearrange("p (b k h v) -> p b h v k", b=BLK, k=2, h=2)
                for h in range(2):
                    last = nc.vector.tensor_reduce(ov[:, p % 2, :, h, :], sums[:, :, h, 0:HD + 1, :], AX.X, ALU.add)
                    if h == 0:
                        last.then_inc(ov_done, 1)
                last.then_inc(misc_taken, 1)
                dve.wait_ge(ov_done, PAIRS * b + p + 1)
                dve.wait_ge(misc_taken, misc_use(w, name) + 1)
                nc.vector.reciprocal(orec[:, p % 2, :, :], ov[:, p % 2, :, :, HD]).then_inc(orec_done, 1)
                dve.wait_ge(orec_done, PAIRS * b + p + 1)
                nc.vector.tensor_tensor(o_tok[:, :, 2 * p * HD:2 * (p + 1) * HD].rearrange("p b (h d) -> p b h d", h=2),
                                        ov[:, p % 2, :, :, 0:HD],
                                        orec[:, p % 2, :, :].unsqueeze(3).to_broadcast([P, BLK, 2, HD]),
                                        ALU.mult).then_inc(norm_done, 1)

            def late(w, name):
                k = int(name[1])
                if name[0] == "O":
                    dve.wait_ge(oThi_done, DC * (w - 1) + k + 1)
                    nc.vector.tensor_tensor(oT[:, 1, k, :], misc[:], oT[:, 0, k, :].bitcast(F32),
                                            ALU.subtract).then_inc(misc_taken, 1)
                else:
                    if k == 0:
                        dve.wait_ge(acc_in, 16 * (w - 1) + 16)
                    dve.wait_ge(misc_full, misc_use(w, name) + 1)
                    at = slice(2 * k, 2 * k + 2)
                    nc.vector.tensor_tensor(acc[:, at, :], misc[:].rearrange("p (b d) -> p b d", b=2), acc[:, at, :],
                                            ALU.add).then_inc(misc_taken, 1)

            def take_kT(b):
                if isinstance(b, int) and b == 0:
                    ring_wait(dve, ring_taken, WIN0, 0, "kT")
                else:
                    dve.wait_ge(sT_full, BLK * PAIRS * b)
                nc.vector.tensor_copy(kT_cur[:], kT_new[:].bitcast(F32)).then_inc(kT_cur_done, 1)

            def slot(win, b, u, point):
                first = isinstance(b, int) and b == 0
                if u is None:
                    if first:
                        take_kT(0)
                    else:
                        normalise(b, "Tp6", b - 1, 6)
                        normalise(b, "Tp7", b - 1, 7)
                        for name in ("O0", "O1", "P0", "P1"):
                            late(b, name)
                    return
                if point == 1:
                    if u >= 2:
                        normalise(b, f"T{u - 2}", b, u - 2)
                    elif not first:
                        normalise(b, f"Tp{u + 6}", b - 1, u + 6)
                if point == 4 and not first and u in LATE:
                    for name in LATE[u]:
                        late(b, name)
                if point == 4 and u == PAIRS - 1 and not (isinstance(b, int) and b == NB - 1):
                    take_kT(b + 1)

            windows(dve, slot, front)

            def experts(b):
                for c in range(NCH):
                    k = NCH * b + c
                    dve.wait_ge(silu_done, k + 1)
                    dve.wait_ge(up_full, k + 1)
                    dve.wait_ge(hlo_done, NCH * b + max(c - 1, 0))
                    nc.vector.tensor_tensor(hid[:, c % 2, :], up_ps[c % 2], act_g[:, c % 2, :],
                                            ALU.mult).then_inc(gu_done, 1)
                    dve.wait_ge(gu_done, k + 1)
                    dve.wait_ge(wps_full, k + 1)
                    nc.vector.tensor_tensor(hid[:, c % 2, :], hid[:, c % 2, :], wgt_ps[:], ALU.mult).then_inc(hid_done, 1)
                dve.wait_ge(down_used, NCH * b + NCH)
                dve.wait_ge(turn_full, 2 * b)
                nc.vector.tensor_copy(dT[:, 1, :], down_ps[:, 1, :]).then_inc(dT_done, 1)
                dve.wait_ge(acc2_in, 16 * b + 16)
                for half in range(2):
                    dve.wait_ge(turn_full, 2 * b + half + 1)
                    at = slice(2 * half, 2 * half + 2)
                    nc.vector.tensor_tensor(acc2[:, at, :], acc2[:, at, :],
                                            turn_ps[:].rearrange("p (b d) -> p b d", b=2), ALU.add).then_inc(turn_taken, 1)

            experts(0)
            with dve.Fori(1, NB) as b:
                experts(b)

        @block.tensor
        def _(pe):
            def three(dst, stat_hi, stat_lo, mov_hi, mov_lo, first, last):
                pe.matmul(dst, stat_hi, mov_hi, start=first, stop=False)
                pe.matmul(dst, stat_hi, mov_lo, start=False, stop=False)
                return pe.matmul(dst, stat_lo, mov_hi, start=False, stop=last)

            def front(win, j, ahead, name):
                if name in RING_OFF:
                    return
                use, n = ring_use(win, ahead, name)
                bank = ring[use]
                if not (isinstance(n, int) and n == 0):
                    pe.wait_ge(ring_taken[use], n)
                if name.startswith("xT"):
                    c = int(name[2:])
                    pe.wait_ge(xn_done, BLK * j + BLK)
                    if isinstance(j, int) and j == 0:
                        pe.wait_ge(consts_in, 64)
                    for b in range(BLK):
                        mm = pe.transpose(bank[:, b * P:(b + 1) * P], xn[:, b, c * P:(c + 1) * P], identf[:])
                elif name.startswith("proj"):
                    b = int(name[4:])
                    if b == 0:
                        for c in range(DC):
                            if (ring_use(win, ahead, f"xT{c}")[0] - use) % 2:
                                ring_wait(pe, ring_taken, win, ahead, f"xT{c}")
                    if isinstance(j, int) and j == 0:
                        pe.wait_ge(wa_split, 1)
                    at = slice(b * P, (b + 1) * P)
                    for c in range(DC):
                        mm = three(bank[:, 0:NPROJ], xT[:, 0, c, at], xT[:, 1, c, at], wa_hi[:, c, :], wa_lo[:, c, :],
                                   c == 0, c == DC - 1)
                elif name == "kT":
                    pe.wait_ge(ka_done, j + 1)
                    for b in range(BLK):
                        mm = pe.transpose(bank[:, b * P:(b + 1) * P], ka[:, b, :, :].rearrange("p t s -> p (t s)"), identf[:])
                elif name == "wT":
                    pe.wait_ge(w3_done, j + 1)
                    pe.wait_ge(identb_done, 1)
                    for b in range(BLK):
                        mm = pe.transpose(bank[:].bitcast(BF16)[0:3 * E, b * P:(b + 1) * P], w3[:, b, :], identb[:])
                elif name.startswith("q"):
                    with_max = name.startswith("qm")
                    p = int(name[3:] if with_max else name[2:])
                    if with_max:
                        pe.wait_ge(m_done, PAIRS * j + p + 1)
                    elif p % (PAIRS // 2) == 0:
                        pe.wait_ge(qa_done, 2 * j + 2 * p // PAIRS + 1)
                    for b in range(BLK):
                        mm = pe.transpose(bank[:, b * P:(b + 1) * P],
                                          qa[:, b, 2 * p:2 * p + 2, :].rearrange("p h s -> p (h s)"), identf[:])
                else:
                    p, s = map(int, name[1:].split("."))
                    qb, lo = s // 2, HS * (s % 2)
                    if s == 0 and ring_use(win, ahead, f"qT{p}")[0] != use:
                        ring_wait(pe, ring_taken, win, ahead, f"qT{p}")
                    mm = pe.matmul(bank[:], qT[lo:lo + KS, p % 2, qb * P:(qb + 1) * P], kT_new[lo:lo + KS, :],
                                   start=True, stop=True, tile_position=(lo, 0))
                mm.then_inc(ring_full[use], 1)

            def scores(b, u, kb):
                n = BLK * u + kb
                if not (isinstance(b, int) and BLK * PAIRS * b + n < 2):
                    pe.wait_ge(exp_done, BLK * PAIRS * b + n - 1)
                for h in range(2):
                    lo = HS * h
                    mm = pe.matmul(sT[n % 2][:, h, :], kT_cur[lo:lo + KM, kb * P:(kb + 1) * P], qmT[lo:lo + KM, u % 2, :],
                                   start=True, stop=True, tile_position=(lo, 0))
                mm.then_inc(sT_full, 1)

            def probs_v(b, p, kbs):
                if kbs[0] == 0:
                    pe.wait_ge(exp_done, BLK * PAIRS * b + BLK * (p + 1))
                    if not (isinstance(b, int) and PAIRS * b + p == 0):
                        pe.wait_ge(pvs_done, PAIRS * b + p)
                    if p == 0:
                        pe.wait_ge(v_cur_done, b + 1)
                for kb in kbs:
                    for h in range(2):
                        to = 2 * VW * (kb % 2) + VW * h
                        mm = pe.matmul(pv[to:to + VW, :], v_cur[:, kb, :], probs[:, p % 2, kb, h, :],
                                       start=(kb < 2), stop=(kb >= 2), tile_position=(0, to))
                if kbs[-1] == BLK - 1:
                    mm.then_inc(pv_full, 1)

            def misc_free(w, name):
                n = misc_use(w, name)
                if not (isinstance(n, int) and n == 0):
                    pe.wait_ge(misc_taken, n)

            def turn(w, name, b, p):
                pe.wait_ge(pvs_done, PAIRS * b + p + 1)
                misc_free(w, name)
                for k in range(BLK):
                    mm = pe.transpose(misc[:, k * P:(k + 1) * P], pvs[:, p % 2, k * P:(k + 1) * P], identf[:])
                mm.then_inc(misc_full, 1)

            def late(w, name):
                k = int(name[1])
                misc_free(w, name)
                if name[0] == "O":
                    if k == 0:
                        pe.wait_ge(norm_done, PAIRS * w)
                    for b in range(BLK):
                        mm = pe.transpose(misc[:, b * P:(b + 1) * P], o_tok[:, b, k * P:(k + 1) * P], identf[:])
                else:
                    if k == 0:
                        pe.wait_ge(wo_split, 1)
                    for b in range(2):
                        at = slice((2 * k + b) * P, (2 * k + b + 1) * P)
                        for c in range(DC):
                            mm = three(misc[:, b * D:(b + 1) * D], oT[:, 0, c, at], oT[:, 1, c, at],
                                       wo_hi[:, c, :], wo_lo[:, c, :], c == 0, c == DC - 1)
                mm.then_inc(misc_full, 1)

            def slot(win, b, u, point):
                first = isinstance(b, int) and b == 0
                if u is None:
                    if not first:
                        turn(b, "Tp6", b - 1, 6)
                        probs_v(b - 1, 7, (0, 1))
                        probs_v(b - 1, 7, (2, 3))
                        turn(b, "Tp7", b - 1, 7)
                        for name in ("O0", "O1", "P0", "P1"):
                            late(b, name)
                    return
                if point in (0, 2):
                    if point == 0:
                        ring_wait(pe, ring_taken, win, 0, f"qmT{u}")
                        if u == 0:
                            pe.wait_ge(kT_cur_done, b + 1)
                    scores(b, u, point)
                    scores(b, u, point + 1)
                elif point in (1, 3):
                    if not (first and u == 0):
                        probs_v(b if u else b - 1, (u - 1) % PAIRS, (0, 1) if point == 1 else (2, 3))
                    if point == 1:
                        if u >= 2:
                            turn(b, f"T{u - 2}", b, u - 2)
                        elif not first:
                            turn(b, f"Tp{u + 6}", b - 1, u + 6)
                elif not first and u in LATE:
                    for name in LATE[u]:
                        late(b, name)

            windows(pe, slot, front)

            def project(b, c, w_hi, w_lo, dst):
                at = slice(c * P, (c + 1) * P)
                for dc in range(DC):
                    mm = three(dst, w_hi[:, dc, at], w_lo[:, dc, at], xT2[:, 0, dc, :], xT2[:, 1, dc, :],
                               dc == 0, dc == DC - 1)
                return mm

            def down(b, c):
                if c == 0:
                    pe.wait_ge(dT_done, 2 * b)
                pe.wait_ge(hlo_done, NCH * b + c + 1)
                pe.wait_ge(lo_done, order["d", c // GC] + 1)
                for dc in range(DC):
                    at = slice(dc * P, (dc + 1) * P)
                    mm = three(down_ps[:, dc, :], d_hi[:, c, at], d_lo[:, c, at], h_hi[:, c % 2, :], h_lo[:, c % 2, :],
                               c == 0, c == NCH - 1)
                mm.then_inc(down_used, 1)

            for bank in range(2):
                pe.wait_ge(ring_taken[bank], RING0 + RING_PER * (NB - 1) + RING_LAST)
            pe.wait_ge(misc_taken, misc_use(NB, "P1") + 1)
            def experts(b):
                pe.wait_ge(xT2_in, 16 * b + 16)
                for c in range(NCH + 2):
                    if c < NCH:
                        pe.wait_ge(lo_done, order["u", c // GC] + 1)
                        pe.wait_ge(silu_done, NCH * b + max(c - 1, 0))
                        project(b, c, g_hi, g_lo, gate_ps[c % 2][:]).then_inc(gate_full, 1)
                        pe.wait_ge(gu_done, NCH * b + max(c - 1, 0))
                        project(b, c, u_hi, u_lo, up_ps[c % 2]).then_inc(up_full, 1)
                        pe.wait_ge(hid_done, NCH * b + c)
                        pe.matmul(wgt_ps[:], sel_sb[:, c * P:(c + 1) * P], wT3[:, bass.ds(b * T, T)],
                                  start=True, stop=True).then_inc(wps_full, 1)
                    if c >= 2:
                        down(b, c - 2)
                pe.wait_ge(dT_done, 2 * b + 2)
                for half in range(2):
                    pe.wait_ge(turn_taken, 2 * b + half)
                    for k in range(2):
                        at = slice((2 * half + k) * P, (2 * half + k + 1) * P)
                        for dc in range(DC):
                            mm = pe.transpose(turn_ps[:, k * D + dc * P:k * D + (dc + 1) * P], dT[:, dc, at], identf[:])
                    mm.then_inc(turn_full, 1)

            experts(0)
            with pe.Fori(1, NB) as b:
                experts(b)


_INS = ["L0_attn_x", "L0_attn_w_attn", "L0_attn_w_out", "L0_ffn_gate_kernel", "L0_ffn_gate_proj", "L0_ffn_up_proj",
        "L0_ffn_down_proj"]


def _constants():
    pos = np.float32(10000.0) ** ((np.float32(-2.0) * np.arange(0, HD, 2, dtype=np.float32) - np.float32(1.0)) / np.float32(HD))
    angles = np.arange(T, dtype=np.float32)[:, None] * pos[None, :].astype(np.float32)
    c, s = np.cos(angles).astype(np.float32), np.sin(angles).astype(np.float32)

    def tokens_on_partitions(a):
        return np.ascontiguousarray(a.reshape(BLK, P, HD).transpose(1, 0, 2))

    return {
        "cos": tokens_on_partitions(np.concatenate([c, c], 1)),
        "sin": tokens_on_partitions(np.concatenate([-s, s], 1)),
        "ident": np.eye(P, dtype=np.float32),
        "sel": np.tile(np.repeat(np.eye(E, dtype=np.float16), M, axis=1), (3, 1)),
    }


def kernel(**inputs):
    import numpy as _np
    import concourse.bacc as _bacc
    from concourse import mybir as _mybir
    from concourse.bass_utils import run_bass_kernel_spmd as _run

    nc = _bacc.Bacc("TRN2", target_bir_lowering=False, num_devices=1)
    arrays, args = {}, []
    given = {name: _np.ascontiguousarray(inputs[name]) for name in _INS}
    for name, a in {**given, **_constants()}.items():
        arrays[f"in_{name}_dram"] = a
        args.append(nc.dram_tensor(f"in_{name}_dram", a.shape, _mybir.dt.from_np(a.dtype), kind="ExternalInput").ap())
    out = nc.dram_tensor("out_0_dram", (NB, T, D), _mybir.dt.float32, kind="ExternalOutput").ap()
    program(nc, *args, out)
    r = _run(nc, [arrays], core_ids=[0])
    return r.results[0]["out_0_dram"]
```

```python
from contextlib import ExitStack

import numpy as np

import concourse.bass as bass
from concourse import mybir

F32 = mybir.dt.float32
F32R = mybir.dt.float32r
ALU = mybir.AluOpType
ACT = mybir.ActivationFunctionType
AX = mybir.AxisListType

P = 128
NB, T, D = 4, 512, 256
BLK = T // P
DC = D // P
H, HD = 16, 16
HALF = HD // 2
NQK = (H + 1) * HD
NQKV = (H + 2) * HD
E, M, TOPK = 32, 96, 8
NPROJ = NQKV + E
HID = E * M
NCH = HID // P
GE = 4
GH = GE * M
GC = GH // P
NG = E // GE
HS = 64
KS = 3 * HD
KM = KS + 2
WB = 3
PAIRS = H // 2
VW = 32
SCALE = HD ** -0.5
EPS = 1e-5

RINGS = 4
RING_OFF = ("norm", "xn", "rope", "split", "route", "exp", "pv", "m", "div", "lo",
            "kS", "next")


def prologue_steps():
    steps = ["norm", "xn", "xT0", "lo.xT0", "xT1", "lo.xT1", "proj0", "proj1", "proj2", "proj3", "rope0", "rope1", "rope2", "split0",
             "kT", "kS", "next", "qT0", "qT1"]
    steps += [f"S0.{s}" for s in range(2 * BLK)] + ["m0", "split1", "qT2", "route0"]
    steps += [f"S1.{s}" for s in range(2 * BLK)]
    steps.insert(steps.index("S1.5"), "qmT0")
    for n in (1, 2, 3):
        steps.insert(steps.index(f"S1.{2 * n}"), f"route{n}")
    return [(0, name) for name in steps]


SLOT = ["m exp0", "", "exp1", "turn pv.0 exp2", "", "qT exp3 div", "qmT", "", "pv.1"]
SLOT_AHEAD = {"exp": 0, "pv": -1, "turn": -2, "div": -2, "m": 1, "qmT": 1, "qT": 3}
PREPARE = {"norm": (0, 1), "xn": (0, 4), "xT0": (1, 0), "lo.xT0": (1, 0), "xT1": (1, 3), "lo.xT1": (1, 4),
           "proj0": (2, 1), "proj1": (2, 4), "proj2": (2, 6), "proj3": (3, 0), "rope0": (3, 1),
           "rope1": (3, 3), "rope2": (4, 0), "route0": (4, 2), "route1": (4, 4), "route2": (4, 4),
           "split0": (4, 7), "route3": (5, 1), "kT": (5, 3), "kS": (5, 7), "wT": (5, 7), "split1": (7, 2)}
FINISH = {"oT0": (1, 7), "lo.oT0": (1, 7), "oT1": (2, 4), "lo.oT1": (2, 4), "out0": (3, 0),
           "out1": (3, 1)}


def window_plan(first=False, last=False):
    def slot_step(u, step):
        kind = step.rstrip("0123.")
        ahead, pair = divmod(u + SLOT_AHEAD[kind], PAIRS)
        return ahead, step if kind == "exp" else f"{kind}{pair}{step[len(kind):]}"

    slots = []
    for u in range(PAIRS):
        steps = []
        for n, names in enumerate(SLOT):
            steps += [slot_step(u, name) for name in names.split()]
            if n < 2 * BLK:
                steps.append(((u + 2) // PAIRS, f"S{(u + 2) % PAIRS}.{n}"))
            steps += [(1, name) for name, at in PREPARE.items() if at == (u, n)]
            steps += [(-1, name) for name, at in FINISH.items() if at == (u, n)]
        if u == PAIRS - 1:
            steps.append((1, "next"))
        if first and u == 1:
            steps.append((0, "wT"))
        slots.append([(ahead, name) for ahead, name in steps
                      if not (first and ahead < 0) and not (last and ahead > 0)])
    return slots


def on_ring(name):
    return not name.startswith(RING_OFF)


def ring_order(steps, banks=None):
    order, uses = {}, [0] * RINGS
    for place, step in enumerate(st for st in steps if on_ring(st[1])):
        bank = place % RINGS
        if banks and step in banks:
            bank = banks[step][0]
        order[step] = bank, uses[bank], place
        uses[bank] += 1
    return order, uses


PROLOGUE = prologue_steps()
EPILOGUE = ["", "turn6 pv7.0 pv7.1 div6", "turn7 div7", "oT0 lo.oT0", "oT1 lo.oT1", "out0", "out1"]
EPILOGUE = [[(-1, name) for name in names.split()] for names in EPILOGUE]
FIRST_PLAN, PLAN, LAST_PLAN = window_plan(first=True), window_plan(), window_plan(last=True)
ORDER0, USES0 = ring_order(PROLOGUE)
ORDER, USES = ring_order(sum(PLAN, []))
FIRST_ORDER, FIRST_USES = ring_order(sum(FIRST_PLAN, []), ORDER)
LAST_ORDER, LAST_USES = ring_order(sum(LAST_PLAN, []))
END_ORDER, END_USES = ring_order(sum(EPILOGUE, []), {step: (RINGS - 1,) for step in sum(EPILOGUE, [])})
USED0 = [USES0[i] + FIRST_USES[i] - USES[i] for i in range(RINGS)]
ALL_USES = [USED0[i] + USES[i] * (NB - 1) + LAST_USES[i] + END_USES[i] for i in range(RINGS)]


def program(nc, x, w_attn, w_out, gate_kernel, gate_proj, up_proj, down_proj, cos, sin, ident, out):
    down_rows = down_proj.rearrange("e m d -> (e m) d")
    xT_dram = nc.dram_tensor("xT_spill", (NB, P, 2 * DC * T), F32, kind="Internal").ap()
    w_dram = nc.dram_tensor("router_weights", (NB, E, T), F32, kind="Internal").ap()
    acc_dram = nc.dram_tensor("acc_spill", (NB, P, BLK * D), F32, kind="Internal").ap()

    with ExitStack() as ctx:
        def sb(name, shape, dt=F32, where=ctx):
            return where.enter_context(nc.sbuf_tensor(name, shape, dt))

        def psum(name, shape):
            return ctx.enter_context(nc.psum_tensor(name, shape, F32))

        def sems(names):
            return [ctx.enter_context(nc.semaphore(name)) for name in names.split()]

        identf = sb("identf", [P, P])
        stage = sb("stage", [P, 3, DC * GH])
        w_raw = stage[:].rearrange("p s n -> p (s n)")[:, 0:DC * (NPROJ + D)].rearrange("p (c n) -> p c n", c=DC)
        g_hi, g_lo = sb("g_hi", [P, DC, HID], F32R), sb("g_lo", [P, DC, HID], F32R)
        xT2 = sb("xT2", [P, 2, 2, DC, T], F32R)
        xT = xT2[:, 1]

        ph1 = ExitStack()
        cs = sb("cs", [P, 2, BLK, HD], where=ph1)
        wa_hi, wa_lo = (sb(n, [P, DC, NPROJ], F32R, ph1) for n in ("wa_hi", "wa_lo"))
        xs = sb("xs", [P, BLK, D], where=ph1)
        xn = sb("xn", [P, BLK, D], where=ph1)
        bn = sb("bn", [P, BLK, 6], where=ph1)
        mv = sb("mv", [P, BLK, 2], where=ph1)
        veps = sb("veps", [P, BLK], where=ph1)
        rstd = sb("rstd", [P, BLK], where=ph1)
        mhalf = sb("mhalf", [P, BLK], where=ph1)
        qkv = sb("qkv", [P, BLK, NPROJ], where=ph1)
        rot_c = sb("rot_c", [P, BLK, NQK], where=ph1)
        rot_s = sb("rot_s", [P, BLK, NQK], where=ph1)
        ka = sb("ka", [P, BLK, 2, HS], where=ph1)
        v_new = sb("v_new", [P, BLK, VW], where=ph1)
        lmax = sb("lmax", [P, BLK], where=ph1)
        ex = sb("ex", [P, BLK, E], where=ph1)
        top8 = sb("top8", [P, BLK, TOPK], where=ph1)
        rest = sb("rest", [P, BLK, E], where=ph1)
        nsum = sb("nsum", [P, BLK], where=ph1)
        nrec = sb("nrec", [P, BLK], where=ph1)
        wgt = sb("wgt", [P, BLK, E], where=ph1)
        wT = sb("wT", [E, T], where=ph1)
        kT_next = sb("kT_next", [P, T], F32R, ph1)
        kT_new = sb("kT_new", [P, 2, T], F32R, ph1)
        qT = sb("qT", [P, 2, T], F32R, ph1)
        nmax = sb("nmax", [P, 2, BLK, 2], where=ph1)
        qa = sb("qa", [P, BLK, H, HS], where=ph1)
        kT_cur = sb("kT_cur", [P, 2, T], F32R, ph1)
        v_cur = sb("v_cur", [P, BLK, VW], where=ph1)
        qmT = sb("qmT", [P, 2, T], F32R, ph1)
        probs = sb("probs", [P, 2, BLK, 2, T], where=ph1)
        pvs = sb("pvs", [P, 2, T], where=ph1)
        ov = sb("ov", [P, 2, BLK, 2, HD + 1], where=ph1)
        orec = sb("orec", [P, 2, BLK, 2], where=ph1)
        o_tok = sb("o_tok", [P, BLK, D], where=ph1)
        wo_hi, wo_lo = (sb(n, [P, DC, D], F32R, ph1) for n in ("wo_hi", "wo_lo"))
        oT = sb("oT", [P, 2, DC, T], F32R, ph1)
        acc = sb("acc", [P, BLK, D], where=ph1)
        ph1.close()

        wb = sb("wb", [P, WB, T])
        act_g = sb("act_g", [P, 2, T])
        hid = sb("hid", [P, 2, T])
        h_hi, h_lo = sb("h_hi", [P, 2, T], F32R), sb("h_lo", [P, 2, T], F32R)
        ud = sb("ud", [P, NG, 2, 2, DC * GH], F32R)
        dT = sb("dT", [P, DC, T])
        acc2 = sb("acc2", [P, BLK, D])
        ud_early = 3

        def up_w(g, part):
            return ud[:, g, 0, part, :].rearrange("p (c n) -> p c n", c=DC)

        def down_w(g, part):
            return ud[:, g, 1, part, :].rearrange("p (r d) -> p r d", r=GC)

        ring = [psum(f"ring{i}", [P, T]) for i in range(RINGS)]
        sT = [psum(f"sT{i}", [P, T]) for i in range(3)]
        pv = psum("pv", [P, T])
        gate_ps, up_ps, down_ps, turn_ps = ring[0:2], sT[0:2], (ring[2], sT[2]), (ring[RINGS - 1], pv)

        consts_in, w_in, wa_hi_done, wo_hi_done, wa_split, wo_split, fixed = sems(
            "consts_in w_in wa_hi_done wo_hi_done wa_split wo_split fixed")
        (waited_apart,) = sems("waited_apart")
        x_in, bn_done, mv_done, veps_done, rstd_done, xn_done, xThi_done, xT_out = sems(
            "x_in bn_done mv_done veps_done rstd_done xn_done xThi_done xT_out")
        ring_full, ring_taken = (sems(" ".join(f"ring_{what}{i}" for i in range(RINGS))) for what in ("full", "taken"))
        rotc_done, rots_done, rot_done, qhi_done, qa_done, khi_done, ka_done, v_done, kT_new_done, kT_cur_done, v_cur_done = sems(
            "rotc_done rots_done rot_done qhi_done qa_done khi_done ka_done v_done kT_new_done kT_cur_done v_cur_done")
        lmax_done, lsub_done, ex_done, top8_done, rest_done, nsum_done, nrec_done, selneg_done, wgt_done = sems(
            "lmax_done lsub_done ex_done top8_done rest_done nsum_done nrec_done selneg_done wgt_done")
        mhi_done, m_done, rw_out = sems("mhi_done m_done rw_out")
        wb_in = sems(" ".join(f"wb_in{i}" for i in range(WB)))
        rot0_done, ov_done = sems("rot0_done ov_done")
        sT_full, exp_done, pv_full, pvs_done, orec_done, norm_done, oThi_done = sems(
            "sT_full exp_done pv_full pvs_done orec_done norm_done oThi_done")
        acc_in, acc_out = sems("acc_in acc_out")
        stage_in = sems("stage_in0 stage_in1 stage_in2")
        hi_done, lo_done = sems("hi_done lo_done")
        xT2_in, acc2_in, gate_full, up_full, silu_done, gu_done, hid_done, hhi_done, hlo_done = sems(
            "xT2_in acc2_in gate_full up_full silu_done gu_done hid_done hhi_done hlo_done")
        down_used, dT_done, turn_full, turn_taken, out_done = sems(
            "down_used dT_done turn_full turn_taken out_done")

        PRO = (ORDER0, lambda bank: 0, 0)

        def middle(b, back):
            return ORDER, lambda bank: USES[bank] * b + (USED0[bank] - USES[bank] * back), back

        def win_at(b):
            if isinstance(b, int):
                if b == 0:
                    return (FIRST_ORDER, lambda bank: USES0[bank], 0), PRO
                if b == NB - 1:
                    return (LAST_ORDER, lambda bank: USED0[bank] + USES[bank] * b, 0), middle(b, 1)
                if b == NB:
                    return ((END_ORDER, lambda bank: ALL_USES[bank] - END_USES[bank], 0),)
            return middle(b, 0), middle(b, 1)

        def ring_use(win, ahead, name):
            for order_, before, back in win:
                if (ahead + back, name) in order_:
                    bank, n, _ = order_[ahead + back, name]
                    return bank, before(bank) + n
            raise KeyError(name)

        def ring_wait(eng, which, win, ahead, names, but=None):
            latest = {}
            for name in sorted(names.split(), key=lambda name: next(
                    o[ahead + back, name][2] for o, _, back in win if (ahead + back, name) in o)):
                bank, n = ring_use(win, ahead, name)
                latest[bank] = n
            for bank, n in latest.items():
                if bank != but:
                    eng.wait_ge(which[bank], n + 1)

        def windows(eng, step):
            def window(b, plan):
                for u, steps in enumerate(plan):
                    for ahead, name in steps:
                        step(win_at(b), b, u, b + ahead, ahead, name)

            for ahead, name in PROLOGUE:
                step((PRO,), 0, None, 0, ahead, name)
            window(0, FIRST_PLAN)
            with eng.Fori(1, NB - 1) as b:
                window(b, PLAN)
            window(NB - 1, LAST_PLAN)

        def epilogue(step, c):
            if c < len(EPILOGUE):
                for ahead, name in EPILOGUE[c]:
                    step(win_at(NB), NB, None, NB + ahead, ahead, name)

        def chunks(b, n):
            return max(NCH * b + n, 0) if isinstance(b, int) else NCH * b + n

        def wait_apart(eng, semaphore, value):
            eng.wait_ge(semaphore, value)
            eng.sem_inc(waited_apart, 1)

        groups = [("g", g) for g in range(NG)]
        for g in range(NG):
            groups += [("u", g), ("d", g)]
        order = {key: n for n, key in enumerate(groups)}

        def group_at(n):
            kind, g = groups[n]
            raw = stage[:, n % 3, :].rearrange("p (r d) -> p r d", r=GC if kind == "d" else DC)
            if kind == "g":
                return [raw] + [w[:, :, g * GH:(g + 1) * GH] for w in (g_hi, g_lo)]
            return [raw] + [(up_w if kind == "u" else down_w)(g, part) for part in range(2)]

        def rotated(half):
            heads = slice(half * H // 2, (half + 1) * H // 2)
            return rot_c[:].rearrange("p b (h d) -> p b h d", d=HD)[:, :, heads, :], qa[:, :, heads, :]

        rc, rs = (t[:].rearrange("p b (h d) -> p b h d", d=HD) for t in (rot_c, rot_s))
        xv = qkv[:, :, 0:NQK].rearrange("p b (h d) -> p b h d", d=HD)
        k_both = rc[:, :, H, :].unsqueeze(2).to_broadcast([P, BLK, 2, HD])

        def rotate(eng, which, blocks=slice(0, BLK)):
            lo, hi, of = ((0, HD, 0), (0, HALF, HALF), (HALF, HD, 0))[which]
            factor = cs[:, min(which, 1), blocks, lo:hi].unsqueeze(2).to_broadcast(
                [P, blocks.stop - blocks.start, H + 1, hi - lo])
            return eng.tensor_tensor((rs if which else rc)[:, blocks, :, lo:hi], xv[:, blocks, :, of:of + hi - lo], factor,
                                     ALU.mult)

        block = ctx.enter_context(nc.Block())

        @block.sync
        def _(sp):
            def tok(a, b):
                return a[bass.ds(b, 1), :, :].rearrange("o (b p) d -> p (o b) d", p=P)

            def row(a, b):
                return a[bass.ds(b, 1), :, :].rearrange("o p n -> p (o n)")

            def load_x(j):
                sp.wait_ge(xn_done, BLK * j)
                sp.dma_start(xs[:], tok(x, j)).then_inc(x_in, 16)

            def load_group(n):
                kind, g = groups[n]
                if n >= 3:
                    sp.wait_ge(lo_done, n - 2)
                slot = stage[:, n % 3, :]
                if kind == "d":
                    to = slot.rearrange("p (r d) -> p r d", r=GC)
                    rows = down_rows[g * GH:(g + 1) * GH, :].rearrange("(r p) d -> p r d", p=P)
                    sp.dma_start(to[:, 0:2, :], rows[:, 0:2, :]).then_inc(stage_in[n % 3], 16)
                    sp.dma_start(to[:, 2:GC, :], rows[:, 2:GC, :]).then_inc(stage_in[n % 3], 16)
                else:
                    w = gate_proj if kind == "g" else up_proj
                    for c in range(DC):
                        sp.dma_start(slot[:, c * GH:(c + 1) * GH].rearrange("p (e m) -> p e m", e=GE),
                                     w[g * GE:(g + 1) * GE, c * P:(c + 1) * P, :].rearrange("e p m -> p e m")
                                     ).then_inc(stage_in[n % 3], 16)

            def load_residual(i):
                sp.wait_ge(acc_out, 16 * i)
                sp.dma_start(acc[:], tok(x, i)).then_inc(acc_in, 16)

            def flat(xT):
                return xT.rearrange("p a c t -> p (a c t)").bitcast(F32)

            def spill_xT(win, j, ahead):
                ring_wait(sp, ring_taken, win, ahead, "xT0 xT1")
                if isinstance(j, int) and j == 0:
                    sp.dma_start(flat(xT2[:, 0]), flat(xT)).then_inc(xT_out, 16)
                else:
                    sp.dma_start(row(xT_dram, j), flat(xT)).then_inc(xT_out, 16)

            def spill_w(win, j, ahead):
                ring_wait(sp, ring_taken, win, ahead, "wT")
                sp.dma_start(w_dram[bass.ds(j, 1)].rearrange("o e t -> e (o t)"), wT[:]).then_inc(rw_out, 16)

            def spill_acc(i):
                ring_wait(sp, ring_taken, win_at(i + 1), -1, "out0 out1")
                sp.dma_start(row(acc_dram, i), acc[:].rearrange("p b d -> p (b d)")).then_inc(acc_out, 16)

            sp.dma_start(xs[:], tok(x, 0)).then_inc(x_in, 16)
            sp.dma_start(w_raw[:, :, 0:NQKV], w_attn.rearrange("(c p) n -> p c n", p=P)).then_inc(w_in, 16)
            sp.dma_start(w_raw[:, :, NQKV:NPROJ], gate_kernel.rearrange("(c p) n -> p c n", p=P)).then_inc(w_in, 16)
            sp.dma_start(identf[:], ident).then_inc(consts_in, 16)
            sp.dma_start(cs[:, 0, :, :], cos).then_inc(consts_in, 16)
            sp.dma_start(cs[:, 1, :, :], sin).then_inc(consts_in, 16)
            sp.dma_start(w_raw[:, :, NPROJ:NPROJ + D], w_out.rearrange("(c p) n -> p c n", p=P)).then_inc(w_in, 16)
            sp.dma_start(acc[:], tok(x, 0)).then_inc(acc_in, 16)
            load_x(1)
            spill_xT((PRO,), 0, 0)
            sp.wait_ge(wo_split, 1)
            for n in range(4):
                load_group(n)
            load_x(2)
            spill_w(win_at(0), 0, 0)
            spill_xT(win_at(0), 1, 1)
            for n in range(4, NG):
                load_group(n)
            spill_w(win_at(0), 1, 1)
            with sp.Fori(1, NB - 2) as b:
                load_x(b + 2)
                spill_xT(win_at(b), b + 1, 1)
                spill_acc(b - 1)
                load_residual(b)
                spill_w(win_at(b), b + 1, 1)
            spill_xT(win_at(NB - 2), NB - 1, 1)
            spill_acc(NB - 3)
            load_residual(NB - 2)
            spill_w(win_at(NB - 2), NB - 1, 1)
            for n in range(NG, NG + 3):
                load_group(n)
            spill_acc(NB - 2)
            load_residual(NB - 1)

            def load_acc(b):
                sp.wait_ge(out_done, 32 * b)
                sp.dma_start(acc2[:].rearrange("p b d -> p (b d)"), row(acc_dram, b)).then_inc(acc2_in, 16)

            def store(b):
                for half in range(2):
                    sp.wait_ge(turn_taken, 2 * b + half + 1)
                    sp.dma_start(tok(out, b)[:, 2 * half:2 * half + 2, :],
                                 acc2[:, 2 * half:2 * half + 2, :]).then_inc(out_done, 16)

            def load_batch(b):
                sp.wait_ge(up_full, NCH * (b - 1))
                sp.dma_start(xT2[:, bass.ds(b % 2, 1)].rearrange("p o a c t -> p (o a c t)").bitcast(F32),
                             row(xT_dram, b)).then_inc(xT2_in, 16)

            def load_w(b, c):
                sp.wait_ge(hid_done, chunks(b, c - WB + 1))
                border = -(c * P) % M or M
                for lo, hi in ((0, border), (border, P)):
                    e = (c * P + lo) // M
                    sp.dma_start(wb[lo:hi, c % WB, :],
                                 w_dram[bass.ds(b, 1), e, :].to_broadcast([hi - lo, T])).then_inc(wb_in[c % WB], 16)

            sp.wait_ge(xT_out, 16 * NB)
            sp.wait_ge(rw_out, 16 * NB)
            sp.wait_ge(hi_done, NG + 1)
            for c in range(WB):
                load_w(0, c)
            load_batch(1)
            for n in range(NG + 3, NG + 7):
                load_group(n)
            for c in range(WB, NCH):
                load_w(0, c)
                for kind, g in (("u", (c + 7) // GC), ("d", (c + 5) // GC)):
                    n = order.get((kind, g), 0)
                    if n > NG + 6 and GC * g == c + (7 if kind == "u" else 5):
                        load_group(n)
                if c == len(EPILOGUE) - 1:
                    spill_acc(NB - 1)
                if c == len(EPILOGUE) + 2:
                    sp.wait_ge(acc_out, 16 * NB)
                    sp.dma_start(acc2[:].rearrange("p b d -> p (b d)"), row(acc_dram, 0)).then_inc(acc2_in, 16)

            def serve(b):
                for c in range(NCH):
                    load_w(b, c)
                    if c == 1 and not isinstance(b, int):
                        load_batch(b + 1)
                    if c == 6:
                        store(b - 1)
                        load_acc(b)

            with sp.Fori(1, NB - 1) as b:
                serve(b)
            serve(NB - 1)
            store(NB - 1)
            sp.wait_ge(out_done, 32 * NB)

        @block.gpsimd
        def _(pool):
            nc.gpsimd.memset(mhalf[:], -0.5).then_inc(fixed, 1)
            nc.gpsimd.memset(qa[:].rearrange("p b h s -> p (b h) s")[:, :, KS:HS], 0.0).then_inc(fixed, 1)
            kav = ka[:].rearrange("p b t s -> p (b t) s")
            nc.gpsimd.memset(kav[:, :, KS:KM], 1.0).then_inc(fixed, 1)
            nc.gpsimd.memset(kav[:, :, KM:HS], 0.0).then_inc(fixed, 1)
            nc.gpsimd.memset(v_new[:, :, HD:HD + 1], 1.0).then_inc(fixed, 1)
            nc.gpsimd.memset(kT_new[:].bitcast(F32), 0.0).then_inc(fixed, 1)
            nc.gpsimd.memset(kT_cur[:].bitcast(F32), 0.0).then_inc(fixed, 1)
            nc.gpsimd.memset(v_new[:, :, HD + 1:VW], 0.0).then_inc(fixed, 1)

            def step(win, b, u, j, ahead, name):
                if name == "norm":
                    wait_apart(pool, mv_done, BLK * j + BLK)
                    nc.gpsimd.tensor_scalar(veps[:], mv[:, :, 1], EPS, None, ALU.add).then_inc(veps_done, 1)
                    pool.wait_ge(veps_done, j + 1)
                    pool.wait_ge(xn_done, BLK * j)
                    nc.gpsimd.tensor_tensor(rstd[:], veps[:], mhalf[:], ALU.pow).then_inc(rstd_done, 1)
                    if u is None:
                        split_wa()
                elif name.startswith("rope") and u is None:
                    pass
                elif name == "rope0":
                    ring_wait(pool, ring_taken, win, ahead, "proj0 proj1 proj2 proj3")
                    pool.wait_ge(qhi_done, 4 * j)
                    pool.wait_ge(qa_done, 2 * j)
                    rotate(nc.gpsimd, 0).then_inc(rotc_done, 1)
                elif name == "rope1":
                    rotate(nc.gpsimd, 1).then_inc(rots_done, 1)
                    rotate(nc.gpsimd, 2).then_inc(rots_done, 1)
                elif name == "rope2":
                    pool.wait_ge(rotc_done, j)
                    pool.wait_ge(rots_done, 2 * j)
                    nc.gpsimd.tensor_tensor(rot_c[:], rot_c[:], rot_s[:], ALU.add).then_inc(rot_done, 1)
                elif name == "split0" or name == "split1":
                    half = int(name[5:])
                    if half == 0:
                        wait_apart(pool, rot_done, j + 1)
                        nc.gpsimd.tensor_copy(ka[:, :, :, 0:HD].bitcast(F32R), k_both).then_inc(khi_done, 1)
                        nc.gpsimd.tensor_copy(ka[:, :, :, 2 * HD:3 * HD].bitcast(F32R), k_both).then_inc(khi_done, 1)
                        pool.wait_ge(khi_done, 2 * j + 2)
                        nc.gpsimd.tensor_tensor(ka[:, :, :, HD:2 * HD].bitcast(F32R), k_both, ka[:, :, :, 0:HD],
                                                ALU.subtract).then_inc(ka_done, 1)
                    q, parts = rotated(half)
                    pool.wait_ge(qhi_done, 4 * j + 2 * half + 2)
                    nc.gpsimd.tensor_tensor(parts[:, :, :, 2 * HD:3 * HD].bitcast(F32R), q, parts[:, :, :, 0:HD],
                                            ALU.subtract).then_inc(qa_done, 1)
                    if half and u is None:
                        split_wo()
                elif name.startswith("m"):
                    p = int(name[1:])
                    latest = {}
                    for n in range(2 * BLK):
                        bank, k = ring_use(win, ahead, f"S{p}.{n}")
                        latest[bank] = k
                    m_hi, m_lo = qa[:, :, 2 * p:2 * p + 2, KS], qa[:, :, 2 * p:2 * p + 2, KS + 1]
                    for bank, k in latest.items():
                        pool.wait_ge(ring_taken[bank], k + 1)
                    pool.sem_inc(waited_apart, 1)
                    nc.gpsimd.tensor_copy(m_hi.bitcast(F32R), nmax[:, p % 2, :, :]).then_inc(mhi_done, 1)
                    pool.wait_ge(mhi_done, PAIRS * j + p + 1)
                    nc.gpsimd.tensor_tensor(m_lo.bitcast(F32R), nmax[:, p % 2, :, :], m_hi,
                                            ALU.subtract).then_inc(m_done, 1)
                elif name.startswith("div"):
                    p = int(name[3:])
                    pool.wait_ge(orec_done, PAIRS * j + p + 1)
                    nc.gpsimd.tensor_tensor(o_tok[:, :, 2 * p * HD:2 * (p + 1) * HD].rearrange("p b (h d) -> p b h d", h=2),
                                            ov[:, p % 2, :, :, 0:HD],
                                            orec[:, p % 2, :, :].unsqueeze(3).to_broadcast([P, BLK, 2, HD]),
                                            ALU.mult).then_inc(norm_done, 1)
                elif name == "exp3" and isinstance(b, int) and b == 0:
                    split_group(u)
                elif name == "exp1" and isinstance(b, int) and b == NB - 1 and u >= PAIRS - 2:
                    split_group(NG + u - (PAIRS - 2))

            def split_group(n):
                raw, hi, lo = group_at(n)
                pool.wait_ge(hi_done, n + 1)
                nc.gpsimd.tensor_tensor(lo, raw, hi.bitcast(F32), ALU.subtract).then_inc(lo_done, 1)

            def split_wa():
                pool.wait_ge(wa_hi_done, 1)
                nc.gpsimd.tensor_tensor(wa_lo[:], w_raw[:, :, 0:NPROJ], wa_hi[:].bitcast(F32), ALU.subtract).then_inc(wa_split, 1)

            def split_wo():
                pool.wait_ge(wo_hi_done, 1)
                nc.gpsimd.tensor_tensor(wo_lo[:], w_raw[:, :, NPROJ:NPROJ + D], wo_hi[:].bitcast(F32), ALU.subtract).then_inc(wo_split, 1)

            windows(pool, step)

            for c in range(NCH):
                epilogue(step, c)
                g = (c - 1) // GC + 1
                if c and (c - 1) % GC < 2 and g < NG:
                    split_group(order["ud"[(c - 1) % GC], g])

        @block.scalar
        def _(act):
            def take(win, ahead, name, dst, src=None):
                bank, n = ring_use(win, ahead, name)
                act.wait_ge(ring_full[bank], n + 1)
                nc.scalar.activation(dst, ring[bank][:] if src is None else src(ring[bank]), ACT.Copy
                                     ).then_inc(ring_taken[bank], 1)

            def step(win, b, u, j, ahead, name):
                if name.startswith("xT"):
                    c = int(name[2:])
                    bank, n = ring_use(win, ahead, name)
                    act.wait_ge(ring_full[bank], n + 1)
                    act.wait_ge(xT_out, 16 * j)
                    nc.scalar.activation(xT[:, 0, c, :], ring[bank][:], ACT.Copy).then_inc(xThi_done, 1)
                elif name.startswith("proj"):
                    k = int(name[4:])
                    if k == 0:
                        act.wait_ge(rot_done, j)
                        act.wait_ge(lsub_done, j)
                        act.wait_ge(v_done, j)
                    take(win, ahead, name, qkv[:, k, :], lambda bank: bank[:, 0:NPROJ])
                elif name == "rope0":
                    ring_wait(act, ring_taken, win, ahead, "proj0 proj1 proj2 proj3")
                    act.wait_ge(v_cur_done, j)
                    act.wait_ge(fixed, 8)
                    nc.scalar.activation(v_new[:, :, 0:HD], qkv[:, :, NQK:NQKV], ACT.Copy).then_inc(v_done, 1)
                elif name.startswith("split"):
                    half = int(name[5:])
                    q, parts = rotated(half)
                    act.wait_ge(rot_done, j + 1)
                    if ahead:
                        ring_wait(act, ring_full, win, 0, f"qmT{(half + 1) * PAIRS // 2 - 1}")
                    for k in range(2):
                        nc.scalar.activation(parts[:, :, :, k * HD:(k + 1) * HD].bitcast(F32R), q, ACT.Copy
                                             ).then_inc(qhi_done, 1)
                elif name == "route0":
                    act.wait_ge(lsub_done, j + 1)
                    nc.scalar.activation(ex[:], ex[:], ACT.Exp).then_inc(ex_done, 1)
                elif name == "kT":
                    act.wait_ge(kT_cur_done, 2 * j)
                    take(win, ahead, name, kT_next[:])
                elif name == "wT":
                    act.wait_ge(rw_out, 16 * j)
                    take(win, ahead, name, wT[:], lambda bank: bank[0:E, :])
                elif name.startswith("qT"):
                    take(win, ahead, name, qT[:, int(name[2:]) % 2, :])
                elif name.startswith("qmT"):
                    take(win, ahead, name, qmT[:, int(name[3:]) % 2, :])
                elif name.startswith("exp"):
                    exp(b, u, int(name[3:]))
                    if isinstance(b, int) and b == 0 and name == "exp3":
                        split_group(u)
                    elif name == "exp1" and isinstance(b, int) and b == NB - 1 and u >= PAIRS - 2:
                        split_group(NG + u - (PAIRS - 2))
                elif name.startswith("pv") and name.endswith(".1"):
                    p = int(name[2:-2])
                    act.wait_ge(pv_full, PAIRS * j + p + 1)
                    nc.scalar.activation(pvs[:, p % 2, :], pv[:], ACT.Copy).then_inc(pvs_done, 1)
                    if p == PAIRS - 1 and not (isinstance(b, int) and b == NB):
                        take_v(b)
                elif name == "next" and u is None:
                    take_v(0)
                elif name.startswith("oT"):
                    ring_wait(act, ring_full, win, ahead, name)
                    nc.scalar.activation(oT[:, 0, int(name[2:]), :], ring[ring_use(win, ahead, name)[0]][:], ACT.Copy
                                         ).then_inc(oThi_done, 1)

            def exp(b, u, kb):
                if kb == 0:
                    act.wait_ge(pv_full, max(u - 1, 0) if isinstance(b, int) and b == 0 else
                                PAIRS * b + u - 1)
                for h in range(2):
                    m = 2 * (BLK * u + kb) + h
                    act.wait_ge(sT_full, BLK * H * b + m + 1)
                    nc.scalar.activation(probs[:, u % 2, kb, h, :], sT[m % 3][:], ACT.Exp, scale=SCALE).then_inc(exp_done, 1)

            def take_v(b):
                if isinstance(b, int) and b == 0:
                    act.wait_ge(v_done, 1)
                nc.scalar.activation(v_cur[:], v_new[:], ACT.Copy).then_inc(v_cur_done, 1)

            def split_group(n):
                raw, hi, lo = group_at(n)
                act.wait_ge(stage_in[n % 3], 32 * (n // 3 + 1))
                nc.scalar.activation(hi, raw, ACT.Copy).then_inc(hi_done, 1)

            act.wait_ge(consts_in, 48)
            act.wait_ge(w_in, 48)
            nc.scalar.activation(wa_hi[:], w_raw[:, :, 0:NPROJ], ACT.Copy).then_inc(wa_hi_done, 1)
            nc.scalar.activation(wo_hi[:], w_raw[:, :, NPROJ:NPROJ + D], ACT.Copy).then_inc(wo_hi_done, 1)
            windows(act, step)

            def silu(b, c):
                act.wait_ge(gate_full, chunks(b, c + 1))
                act.wait_ge(gu_done, chunks(b, c - 1))
                nc.scalar.activation(act_g[:, c % 2, :], gate_ps[c % 2][:], ACT.Silu).then_inc(silu_done, 1)

            def hidden_hi(b, c):
                act.wait_ge(hid_done, chunks(b, c + 1))
                act.wait_ge(down_used, chunks(b, c - 1))
                nc.scalar.activation(h_hi[:, c % 2, :], hid[:, c % 2, :], ACT.Copy).then_inc(hhi_done, 1)

            def take_sums(b):
                act.wait_ge(down_used, NCH * b + NCH)
                nc.scalar.activation(dT[:, 0, :], down_ps[0][:], ACT.Copy).then_inc(dT_done, 1)

            for c in range(NCH):
                epilogue(step, c)
                if c:
                    hidden_hi(0, c - 1)
                silu(0, c)
                if c:
                    g = (c - 1) // GC + 1
                    if (c - 1) % GC < 2 and g < NG:
                        if g == ud_early and (c - 1) % GC == 0:
                            act.wait_ge(acc_out, 16 * NB)
                        split_group(order["ud"[(c - 1) % GC], g])
            with act.Fori(1, NB) as b:
                for c in range(NCH):
                    if c == 2:
                        take_sums(b - 1)
                    hidden_hi(b - (c == 0), (c - 1) % NCH)
                    silu(b, c)
            hidden_hi(NB - 1, NCH - 1)
            take_sums(NB - 1)

        @block.vector
        def _(dve):
            def step(win, b, u, j, ahead, name):
                if name == "norm":
                    dve.wait_ge(x_in, 16 * j + 16)
                    for k in range(BLK):
                        nc.vector.bn_stats(bn[:, k, :], xs[:, k, :]).then_inc(bn_done, 1)
                    dve.wait_ge(xn_done, BLK * j)
                    wait_apart(dve, bn_done, BLK * j + BLK)
                    for k in range(BLK):
                        nc.vector.bn_aggr(mv[:, k, :], bn[:, k, :]).then_inc(mv_done, 1)
                elif name == "xn":
                    dve.wait_ge(rstd_done, j + 1)
                    for k in range(BLK):
                        nc.vector.tensor_scalar(xn[:, k, :], xs[:, k, :], mv[:, k, 0:1], rstd[:, k:k + 1],
                                                ALU.subtract, ALU.mult).then_inc(xn_done, 1)
                elif name.startswith("lo.xT"):
                    c, bank = int(name[5:]), ring_use(win, ahead, name[3:])[0]
                    dve.wait_ge(xThi_done, DC * j + c + 1)
                    nc.vector.tensor_tensor(xT[:, 1, c, :], ring[bank][:], xT[:, 0, c, :].bitcast(F32),
                                            ALU.subtract).then_inc(ring_taken[bank], 1)
                elif name == "route0":
                    logits = qkv[:, :, NQKV:NPROJ]
                    ring_wait(dve, ring_taken, win, ahead, "proj0 proj1 proj2 proj3")
                    if ahead:
                        ring_wait(dve, ring_full, win, 0, "wT")
                    nc.vector.tensor_reduce(lmax[:], logits, AX.X, ALU.max).then_inc(lmax_done, 1)
                    dve.wait_ge(lmax_done, j + 1)
                    nc.vector.tensor_tensor(ex[:], logits, lmax[:].unsqueeze(2).to_broadcast([P, BLK, E]),
                                            ALU.subtract).then_inc(lsub_done, 1)
                elif name == "route1":
                    wait_apart(dve, ex_done, j + 1)
                    for k in range(BLK):
                        nc.vector.max(top8[:, k, :], ex[:, k, :]).then_inc(top8_done, 1)
                elif name == "route2":
                    wait_apart(dve, top8_done, BLK * j + BLK)
                    for k in range(BLK):
                        nc.vector.match_replace(out=rest[:, k, :], in_to_replace=top8[:, k, :], in_values=ex[:, k, :],
                                                imm_value=-1.0).then_inc(rest_done, 1)
                    nc.vector.tensor_reduce(nsum[:], top8[:], AX.X, ALU.add, negate=True).then_inc(nsum_done, 1)
                elif name == "route3":
                    dve.wait_ge(nsum_done, j + 1)
                    nc.vector.reciprocal(nrec[:], nsum[:]).then_inc(nrec_done, 1)
                    dve.wait_ge(rest_done, BLK * j + BLK)
                    nc.vector.scalar_tensor_tensor(out=wgt[:], in0=rest[:], scalar=0.0, in1=ex[:], op0=ALU.max,
                                                   op1=ALU.subtract).then_inc(selneg_done, 1)
                    dve.wait_ge(nrec_done, j + 1)
                    dve.wait_ge(selneg_done, j + 1)
                    nc.vector.tensor_tensor(wgt[:], wgt[:], nrec[:].unsqueeze(2).to_broadcast([P, BLK, E]),
                                            ALU.mult).then_inc(wgt_done, 1)
                elif name.startswith("S"):
                    p, s = map(int, name[1:].split("."))
                    bank, n = ring_use(win, ahead, name)
                    if s == 0 and not (isinstance(j, int) and PAIRS * j + p < 2):
                        dve.wait_ge(m_done, PAIRS * j + p - 1)
                    dve.wait_ge(ring_full[bank], n + 1)
                    nc.vector.tensor_reduce(nmax[:, p % 2, s // 2, s % 2:s % 2 + 1], ring[bank][:], AX.X, ALU.max,
                                            negate=True).then_inc(ring_taken[bank], 1)
                elif name.startswith("turn"):
                    p = int(name[4:])
                    bank, n = ring_use(win, ahead, name)
                    if not (isinstance(j, int) and PAIRS * j + p < 2):
                        dve.wait_ge(norm_done, PAIRS * j + p - 1)
                    dve.wait_ge(ring_full[bank], n + 1)
                    sums = ring[bank][:].rearrange("p (b k h v) -> p b h v k", b=BLK, k=2, h=2)
                    for h in range(2):
                        last = nc.vector.tensor_reduce(ov[:, p % 2, :, h, :], sums[:, :, h, 0:HD + 1, :], AX.X, ALU.add)
                        if h == 0:
                            last.then_inc(ov_done, 1)
                    last.then_inc(ring_taken[bank], 1)
                elif name.startswith("div"):
                    p = int(name[3:])
                    dve.wait_ge(ov_done, PAIRS * j + p + 1)
                    ring_wait(dve, ring_taken, win, ahead, f"turn{p}")
                    nc.vector.reciprocal(orec[:, p % 2, :, :], ov[:, p % 2, :, :, HD]).then_inc(orec_done, 1)
                elif name.startswith("lo.oT"):
                    k, bank = int(name[5:]), ring_use(win, ahead, name[3:])[0]
                    dve.wait_ge(oThi_done, DC * j + k + 1)
                    nc.vector.tensor_tensor(oT[:, 1, k, :], ring[bank][:], oT[:, 0, k, :].bitcast(F32),
                                            ALU.subtract).then_inc(ring_taken[bank], 1)
                elif name.startswith("out"):
                    k, bank = int(name[3:]), ring_use(win, ahead, name)[0]
                    if k == 0:
                        dve.wait_ge(acc_in, 16 * j + 16)
                    ring_wait(dve, ring_full, win, ahead, name)
                    at = slice(2 * k, 2 * k + 2)
                    nc.vector.tensor_tensor(acc[:, at, :], ring[bank][:].rearrange("p (b d) -> p b d", b=2), acc[:, at, :],
                                            ALU.add).then_inc(ring_taken[bank], 1)
                elif name == "rope0" and u is None:
                    for k in range(BLK):
                        ring_wait(dve, ring_taken, win, ahead, f"proj{k}")
                        for which in range(3):
                            rotate(nc.vector, which, slice(k, k + 1)).then_inc(rot0_done, 1)
                        dve.wait_ge(rot0_done, 3 * k + 3)
                        last = nc.vector.tensor_tensor(rot_c[:, k, :], rot_c[:, k, :], rot_s[:, k, :], ALU.add)
                    last.then_inc(rot_done, 1)
                elif name == "kS":
                    ring_wait(dve, ring_taken, win, ahead, "kT")
                    if isinstance(j, int) and j == 0:
                        dve.wait_ge(fixed, 8)
                    for h in range(2):
                        rows = slice(HS * h, HS * h + KS)
                        nc.vector.tensor_copy(kT_new[rows, h, :], kT_next[rows, :].bitcast(F32)).then_inc(kT_new_done, 1)
                elif name == "next":
                    if u is not None:
                        dve.wait_ge(sT_full, BLK * H * j)
                    for h in range(2):
                        rows = slice(HS * h, HS * h + HS)
                        nc.vector.tensor_copy(kT_cur[rows, h, :], kT_next[rows, :].bitcast(F32)).then_inc(kT_cur_done, 1)

            windows(dve, step)

            def hidden(b, c):
                dve.wait_ge(silu_done, chunks(b, c + 1))
                dve.wait_ge(up_full, chunks(b, c + 1))
                dve.wait_ge(hlo_done, chunks(b, c - 1))
                nc.vector.tensor_tensor(hid[:, c % 2, :], up_ps[c % 2][:], act_g[:, c % 2, :], ALU.mult).then_inc(gu_done, 1)
                dve.wait_ge(gu_done, chunks(b, c + 1))
                dve.wait_ge(wb_in[c % WB], 32 * (NCH // WB * b + c // WB + 1))
                nc.vector.tensor_tensor(hid[:, c % 2, :], hid[:, c % 2, :], wb[:, c % WB, :], ALU.mult).then_inc(hid_done, 1)

            def hidden_lo(b, c):
                dve.wait_ge(hhi_done, chunks(b, c + 1))
                dve.wait_ge(down_used, chunks(b, c - 1))
                nc.vector.tensor_tensor(h_lo[:, c % 2, :], hid[:, c % 2, :], h_hi[:, c % 2, :].bitcast(F32),
                                        ALU.subtract).then_inc(hlo_done, 1)

            def take_sums(b):
                dve.wait_ge(down_used, NCH * b + NCH)
                nc.vector.tensor_copy(dT[:, 1, :], down_ps[1][:]).then_inc(dT_done, 1)

            def add(b, half):
                if half == 0:
                    dve.wait_ge(acc2_in, 16 * b + 16)
                dve.wait_ge(turn_full, 2 * b + half + 1)
                at = slice(2 * half, 2 * half + 2)
                nc.vector.tensor_tensor(acc2[:, at, :], acc2[:, at, :],
                                        turn_ps[half][:].rearrange("p (b d) -> p b d", b=2), ALU.add).then_inc(turn_taken, 1)

            for c in range(NCH):
                epilogue(step, c)
                hidden(0, c)
                hidden_lo(0, c)
            with dve.Fori(1, NB) as b:
                for c in range(NCH):
                    if c == 2:
                        take_sums(b - 1)
                    elif c in (3, 4):
                        add(b - 1, c - 3)
                    hidden(b, c)
                    hidden_lo(b, c)
            take_sums(NB - 1)
            add(NB - 1, 0)
            add(NB - 1, 1)

        @block.tensor
        def _(pe):
            def three(dst, stat_hi, stat_lo, mov_hi, mov_lo, first, last):
                pe.matmul(dst, stat_hi, mov_hi, start=first, stop=False)
                pe.matmul(dst, stat_hi, mov_lo, start=False, stop=False)
                return pe.matmul(dst, stat_lo, mov_hi, start=False, stop=last)

            def step(win, b, u, j, ahead, name):
                if not on_ring(name):
                    if name.startswith("exp"):
                        scores(win, b, u, int(name[3:]))
                    elif name.startswith("pv"):
                        probs_v(j, int(name[2:-2]), int(name[-1]))
                    return
                use, n = ring_use(win, ahead, name)
                bank = ring[use]
                if not (isinstance(n, int) and n == 0):
                    pe.wait_ge(ring_taken[use], n)
                if name.startswith("xT"):
                    c = int(name[2:])
                    pe.wait_ge(xn_done, BLK * j + BLK)
                    if isinstance(j, int) and j == 0:
                        pe.wait_ge(consts_in, 48)
                    for k in range(BLK):
                        mm = pe.transpose(bank[:, k * P:(k + 1) * P], xn[:, k, c * P:(c + 1) * P], identf[:])
                elif name.startswith("proj"):
                    k = int(name[4:])
                    if k == 0:
                        ring_wait(pe, ring_taken, win, ahead, "xT0 xT1", but=use)
                    if isinstance(j, int) and j == 0:
                        pe.wait_ge(wa_split, 1)
                    at = slice(k * P, (k + 1) * P)
                    for c in range(DC):
                        mm = three(bank[:, 0:NPROJ], xT[:, 0, c, at], xT[:, 1, c, at], wa_hi[:, c, :], wa_lo[:, c, :],
                                   c == 0, c == DC - 1)
                elif name == "kT":
                    pe.wait_ge(ka_done, j + 1)
                    for k in range(BLK):
                        mm = pe.transpose(bank[:, k * P:(k + 1) * P], ka[:, k, :, :].rearrange("p t s -> p (t s)"), identf[:])
                elif name == "wT":
                    pe.wait_ge(wgt_done, j + 1)
                    for k in range(BLK):
                        mm = pe.transpose(bank[0:E, k * P:(k + 1) * P], wgt[:, k, :], identf[:])
                elif name.startswith("q"):
                    with_max = name.startswith("qm")
                    p = int(name[3:] if with_max else name[2:])
                    if with_max:
                        pe.wait_ge(m_done, PAIRS * j + p + 1)
                    elif p % (PAIRS // 2) == 0:
                        pe.wait_ge(qa_done, 2 * j + 2 * p // PAIRS + 1)
                    for k in range(BLK):
                        mm = pe.transpose(bank[:, k * P:(k + 1) * P],
                                          qa[:, k, 2 * p:2 * p + 2, :].rearrange("p h s -> p (h s)"), identf[:])
                elif name.startswith("turn"):
                    p = int(name[4:])
                    pe.wait_ge(pvs_done, PAIRS * j + p + 1)
                    for k in range(BLK):
                        mm = pe.transpose(bank[:, k * P:(k + 1) * P], pvs[:, p % 2, k * P:(k + 1) * P], identf[:])
                elif name.startswith("oT"):
                    c = int(name[2:])
                    if c == 0:
                        pe.wait_ge(norm_done, PAIRS * j + PAIRS)
                    for k in range(BLK):
                        mm = pe.transpose(bank[:, k * P:(k + 1) * P], o_tok[:, k, c * P:(c + 1) * P], identf[:])
                elif name.startswith("out"):
                    half = int(name[3:])
                    if half == 0:
                        pe.wait_ge(wo_split, 1)
                        ring_wait(pe, ring_taken, win, ahead, "oT0 oT1", but=use)
                    for k in range(2):
                        at = slice((2 * half + k) * P, (2 * half + k + 1) * P)
                        for c in range(DC):
                            mm = three(bank[:, k * D:(k + 1) * D], oT[:, 0, c, at], oT[:, 1, c, at],
                                       wo_hi[:, c, :], wo_lo[:, c, :], c == 0, c == DC - 1)
                else:
                    p, s = map(int, name[1:].split("."))
                    qb = s // 2
                    if s == 0:
                        ring_wait(pe, ring_taken, win, ahead, f"qT{p}", but=use)
                        if p == 0:
                            pe.wait_ge(kT_new_done, 2 * j + 2)
                    mm = pe.matmul(bank[:], qT[:, p % 2, qb * P:(qb + 1) * P], kT_new[:, s % 2, :], start=True, stop=True)
                mm.then_inc(ring_full[use], 1)

            def scores(win, b, u, kb):
                if kb == 0:
                    ring_wait(pe, ring_taken, win, 0, f"qmT{u}")
                    if u == 0:
                        pe.wait_ge(kT_cur_done, 2 * b + 2)
                for h in range(2):
                    m = 2 * (BLK * u + kb) + h
                    if m >= 3:
                        pe.wait_ge(exp_done, BLK * H * b + m - 2)
                    elif m == 0 and not (isinstance(b, int) and b == 0):
                        pe.wait_ge(exp_done, BLK * H * b)
                    pe.matmul(sT[m % 3][:], kT_cur[:, h, kb * P:(kb + 1) * P], qmT[:, u % 2, :], start=True, stop=True
                              ).then_inc(sT_full, 1)

            def probs_v(b, p, half):
                kbs = (2 * half, 2 * half + 1)
                if half == 0:
                    pe.wait_ge(exp_done, BLK * H * b + 2 * BLK * (p + 1))
                    if not (isinstance(b, int) and PAIRS * b + p == 0):
                        pe.wait_ge(pvs_done, PAIRS * b + p)
                    if p == 0:
                        pe.wait_ge(v_cur_done, b + 1)
                for kb in kbs:
                    for h in range(2):
                        to = 2 * VW * (kb % 2) + VW * h
                        mm = pe.matmul(pv[to:to + VW, :], v_cur[:, kb, :], probs[:, p % 2, kb, h, :],
                                       start=(kb < 2), stop=(kb >= 2), tile_position=(0, to))
                if half:
                    mm.then_inc(pv_full, 1)

            windows(pe, step)

            def project(b, c, w_hi, w_lo, dst):
                for dc in range(DC):
                    mm = three(dst, w_hi(dc), w_lo(dc), *(xT2[:, bass.ds(b % 2, 1), part, dc, :].rearrange("p o t -> p (o t)")
                                                          for part in range(2)), dc == 0, dc == DC - 1)
                return mm

            def chunk(b, c):
                first = isinstance(b, int)
                g, at, at_g = c // GC, slice(c * P, (c + 1) * P), slice(c % GC * P, (c % GC + 1) * P)
                if first and c < 2:
                    pe.wait_ge(ring_taken[c], ALL_USES[c])
                pe.wait_ge(silu_done, chunks(b, c - 1))
                project(b, c, lambda dc: g_hi[:, dc, at], lambda dc: g_lo[:, dc, at], gate_ps[c % 2][:]
                        ).then_inc(gate_full, 1)
                if first:
                    pe.wait_ge(lo_done, order["u", g] + 1)
                    if c == 0:
                        pe.wait_ge(exp_done, BLK * H * NB)
                pe.wait_ge(gu_done, chunks(b, c - 1))
                project(b, c, lambda dc: up_w(g, 0)[:, dc, at_g], lambda dc: up_w(g, 1)[:, dc, at_g], up_ps[c % 2][:]
                        ).then_inc(up_full, 1)

            def down(b, c, loaded=True):
                g, r = divmod(c, GC)
                if not loaded and c == 0:
                    pe.wait_ge(ring_taken[2], ALL_USES[2])
                pe.wait_ge(hlo_done, NCH * b + c + 1)
                if not loaded:
                    pe.wait_ge(lo_done, order["d", g] + 1)
                for dc in range(DC):
                    at = slice(dc * P, (dc + 1) * P)
                    mm = three(down_ps[dc][:], down_w(g, 0)[:, r, at], down_w(g, 1)[:, r, at], h_hi[:, c % 2, :],
                               h_lo[:, c % 2, :], c == 0, c == NCH - 1)
                mm.then_inc(down_used, 1)

            def turn_sums(b, half):
                if half == 0:
                    pe.wait_ge(dT_done, 2 * b + 2)
                for k in range(2):
                    at = slice((2 * half + k) * P, (2 * half + k + 1) * P)
                    for dc in range(DC):
                        mm = pe.transpose(turn_ps[half][:, k * D + dc * P:k * D + (dc + 1) * P], dT[:, dc, at], identf[:])
                mm.then_inc(turn_full, 1)

            pe.wait_ge(xT_out, 16)
            for c in range(NCH):
                epilogue(step, c)
                chunk(0, c)
                if c >= 2:
                    down(0, c - 2, loaded=False)
            pe.wait_ge(ring_taken[RINGS - 1], ALL_USES[RINGS - 1])
            pe.wait_ge(pvs_done, PAIRS * NB)
            with pe.Fori(1, NB) as b:
                pe.wait_ge(xT2_in, 16 * b)
                for c in range(NCH):
                    chunk(b, c)
                    if c == 2:
                        turn_sums(b - 1, 0)
                        down(b, 0)
                        turn_sums(b - 1, 1)
                    elif c < 2:
                        down(b - 1, NCH - 2 + c)
                    else:
                        down(b, c - 2)
            down(NB - 1, NCH - 2)
            down(NB - 1, NCH - 1)
            turn_sums(NB - 1, 0)
            turn_sums(NB - 1, 1)


_INS = ["L0_attn_x", "L0_attn_w_attn", "L0_attn_w_out", "L0_ffn_gate_kernel", "L0_ffn_gate_proj", "L0_ffn_up_proj",
        "L0_ffn_down_proj"]


def _constants():
    pos = np.float32(10000.0) ** ((np.float32(-2.0) * np.arange(0, HD, 2, dtype=np.float32) - np.float32(1.0)) / np.float32(HD))
    angles = np.arange(T, dtype=np.float32)[:, None] * pos[None, :].astype(np.float32)
    c, s = np.cos(angles).astype(np.float32), np.sin(angles).astype(np.float32)

    def tokens_on_partitions(a):
        return np.ascontiguousarray(a.reshape(BLK, P, HD).transpose(1, 0, 2))

    return {
        "cos": tokens_on_partitions(np.concatenate([c, c], 1)),
        "sin": tokens_on_partitions(np.concatenate([-s, s], 1)),
        "ident": np.eye(P, dtype=np.float32),
    }


def kernel(**inputs):
    import numpy as _np
    import concourse.bacc as _bacc
    from concourse import mybir as _mybir
    from concourse.bass_utils import run_bass_kernel_spmd as _run

    nc = _bacc.Bacc("TRN2", target_bir_lowering=False, num_devices=1)
    arrays, args = {}, []
    given = {name: _np.ascontiguousarray(inputs[name]) for name in _INS}
    for name, a in {**given, **_constants()}.items():
        arrays[f"in_{name}_dram"] = a
        args.append(nc.dram_tensor(f"in_{name}_dram", a.shape, _mybir.dt.from_np(a.dtype), kind="ExternalInput").ap())
    out = nc.dram_tensor("out_0_dram", (NB, T, D), _mybir.dt.float32, kind="ExternalOutput").ap()
    program(nc, *args, out)
    r = _run(nc, [arrays], core_ids=[0])
    return r.results[0]["out_0_dram"]
```
